# Optimizing a Trainium2 kernel written in Bass

```python
import numpy as np
import jax
import jax.numpy as jnp

def _softmax(x, axis=-1):
    return jax.nn.softmax(x, axis=axis)

def _gelu(x):
    return jax.nn.gelu(x, approximate=True)

def _silu(x):
    return jax.nn.silu(x)

def _sigmoid(x):
    return jax.nn.sigmoid(x)

def _layernorm(x, axis=-1, eps=1e-05):
    m = jnp.mean(x, axis=axis, keepdims=True)
    v = jnp.var(x, axis=axis, keepdims=True)
    return (x - m) / jnp.sqrt(v + eps)

def _scatter_add(tgt, idx, src, axis=0):
    return tgt.at[idx].add(src)

def _segment_sum(src, seg, n):
    return jax.ops.segment_sum(src, seg, n)
kernel_name = 'mk_seq_preln_d2_jaxref_r8_9edeec'

def setup_inputs(seed: int=0):
    np.random.seed(seed)
    _w = jnp.asarray

    def _L0_attn_setup():
        import jax, jax.numpy as jnp
        import numpy as np
        B, T, D_MODEL = (2, 64, 128)
        D_INNER, D_HEAD, D_CONV = (256, 64, 4)
        N_HEADS, D_STATE = (32, 32)
        DT_MIN, DT_MAX, K_MAX, EPS = (0.0001, 0.1, 0.5, 1e-08)

        def _forward(x, W_in, dw_weight, dw_bias, W_bc, W_out, skip, A_log, dt_bias):
            Bsz, Tlen, D = x.shape
            DI, K = dw_weight.shape
            H, N = A_log.shape
            DH = DI // H
            proj = jnp.einsum('btd,od->bto', x, W_in)
            gate = proj[..., :DI]
            value_raw = proj[..., DI:2 * DI]
            params = proj[..., 2 * DI:].reshape(Bsz, Tlen, H, 2)
            xp = jnp.pad(value_raw, ((0, 0), (K - 1, 0), (0, 0)))
            conv = dw_bias + sum((xp[:, k:k + Tlen, :] * dw_weight[:, k] for k in range(K)))
            value = jax.nn.silu(conv)
            dt = jnp.clip(jax.nn.softplus(params[..., 0] + dt_bias), DT_MIN, DT_MAX)
            kd = K_MAX * jax.nn.sigmoid(params[..., 1])
            A = jnp.exp(A_log)
            bc = jnp.einsum('bti,oi->bto', value, W_bc).reshape(Bsz, Tlen, H, 4, N)
            bc = bc / (jnp.sqrt(jnp.sum(bc * bc, axis=-1, keepdims=True)) + EPS)
            Bz, Bx, Cz, Cx = (bc[..., 0, :], bc[..., 1, :], bc[..., 2, :], bc[..., 3, :])
            u = value.reshape(Bsz, Tlen, H, DH)

            def step(carry, inp):
                z, s = carry
                u_t, dt_t, k_t, Bz_t, Bx_t, Cz_t, Cx_t = inp
                dtE = dt_t[:, :, None, None]
                S = 1.0 / (1.0 + dt_t[..., None] * k_t[..., None] + (dt_t * dt_t)[..., None] * A)
                z = S[..., None] * (z - dtE * A[None, :, :, None] * s + dtE * (Bz_t[..., None] * u_t[:, :, None, :]))
                s = s + dtE * z + dtE * (Bx_t[..., None] * u_t[:, :, None, :])
                y = jnp.einsum('bhn,bhnd->bhd', Cz_t, z) + jnp.einsum('bhn,bhnd->bhd', Cx_t, s)
                return ((z, s), y)
            tm = lambda a: jnp.moveaxis(a, 1, 0)
            init = (jnp.zeros((Bsz, H, N, DH), x.dtype), jnp.zeros((Bsz, H, N, DH), x.dtype))
            _, ys = jax.lax.scan(step, init, (tm(u), tm(dt), tm(kd), tm(Bz), tm(Bx), tm(Cz), tm(Cx)))
            y = jnp.moveaxis(ys, 0, 1).reshape(Bsz, Tlen, DI)
            y = (y + skip * value) * jax.nn.silu(gate)
            return jnp.einsum('bti,oi->bto', y, W_out)
        key = jax.random.key(seed)
        ks = jax.random.split(key, 8)
        n = lambda k, sh, s=1.0: jax.random.normal(k, sh, jnp.float32) * s
        return {'x': n(ks[0], (B, T, D_MODEL)), 'W_in': n(ks[1], (2 * D_INNER + N_HEADS * 2, D_MODEL), D_MODEL ** (-0.5)), 'dw_weight': n(ks[2], (D_INNER, D_CONV), D_CONV ** (-0.5)), 'dw_bias': n(ks[3], (D_INNER,), 0.1), 'W_bc': n(ks[4], (N_HEADS * 4 * D_STATE, D_INNER), D_INNER ** (-0.5)), 'W_out': n(ks[5], (D_MODEL, D_INNER), D_INNER ** (-0.5)), 'skip': jnp.ones((D_INNER,), jnp.float32), 'A_log': n(ks[6], (N_HEADS, D_STATE), 0.5), 'dt_bias': n(ks[7], (N_HEADS,), 0.5)}
    _L0_attn_in = _L0_attn_setup()

    def _L0_ffn_setup():
        import jax, jax.numpy as jnp
        import numpy as np
        D_IN, D_HID = (128, 512)

        def _ternary(key, shape):
            return jax.random.randint(key, shape, -1, 2).astype(jnp.float32)

        def _tlin(x, w, s):
            return jnp.einsum('bsi,oi->bso', x, w) * s
        key = jax.random.key(seed)
        ks = jax.random.split(key, 12)
        inv = lambda fan: 1.0 / np.sqrt(fan).astype(np.float32)
        return {'x': jax.random.normal(ks[0], (4, 256, D_IN), dtype=jnp.float32), 'w1_w': _ternary(ks[1], (D_HID, D_IN)), 'w1_s': jax.random.uniform(ks[2], (D_HID,), dtype=jnp.float32) * inv(D_IN), 'w2_w': _ternary(ks[3], (D_HID, D_IN)), 'w2_s': jax.random.uniform(ks[4], (D_HID,), dtype=jnp.float32) * inv(D_IN), 'h1_w': _ternary(ks[5], (D_HID, D_HID)), 'h1_s': jax.random.uniform(ks[6], (D_HID,), dtype=jnp.float32) * inv(D_HID), 'h2_w': _ternary(ks[7], (D_HID, D_HID)), 'h2_s': jax.random.uniform(ks[8], (D_HID,), dtype=jnp.float32) * inv(D_HID), 'w3_w': _ternary(ks[9], (D_IN, D_HID)), 'w3_s': jax.random.uniform(ks[10], (D_IN,), dtype=jnp.float32) * inv(D_HID)}
    _L0_ffn_in = _L0_ffn_setup()

    def _L1_attn_setup():
        import jax, jax.numpy as jnp
        import numpy as np
        DIM = 128
        HEADS = 16
        DIM_HEAD = 64
        DIM_INNER = HEADS * DIM_HEAD
        SCALE = DIM_HEAD ** (-0.5)

        def rmsnorm(x, w):
            eps = jnp.asarray(jnp.finfo(x.dtype).eps, x.dtype)
            var = jnp.mean(jnp.square(x), axis=-1, keepdims=True)
            return x * jax.lax.rsqrt(var + eps) * w
        key = jax.random.key(seed)
        ks = jax.random.split(key, 6)
        tokens = jax.random.normal(ks[0], (2, 256, DIM), dtype=jnp.float32)
        norm_w = jnp.ones((DIM,), dtype=jnp.float32)
        Wq = jax.random.normal(ks[1], (DIM, DIM_INNER), dtype=jnp.float32) * 0.02
        Wkv = jax.random.normal(ks[2], (DIM, 2 * DIM_INNER), dtype=jnp.float32) * 0.02
        Wout = jax.random.normal(ks[3], (DIM_INNER, DIM), dtype=jnp.float32) * 0.02
        Wg = jax.random.normal(ks[4], (DIM, HEADS), dtype=jnp.float32) * 0.02
        return {'tokens': tokens, 'norm_w': norm_w, 'Wq': Wq, 'Wkv': Wkv, 'Wout': Wout, 'Wg': Wg}
    _L1_attn_in = _L1_attn_setup()

    def _L1_ffn_setup():
        import jax, jax.numpy as jnp
        import numpy as np
        D_IN, D_HID = (128, 512)

        def _ternary(key, shape):
            return jax.random.randint(key, shape, -1, 2).astype(jnp.float32)

        def _tlin(x, w, s):
            return jnp.einsum('bsi,oi->bso', x, w) * s
        key = jax.random.key(seed)
        ks = jax.random.split(key, 12)
        inv = lambda fan: 1.0 / np.sqrt(fan).astype(np.float32)
        return {'x': jax.random.normal(ks[0], (4, 256, D_IN), dtype=jnp.float32), 'w1_w': _ternary(ks[1], (D_HID, D_IN)), 'w1_s': jax.random.uniform(ks[2], (D_HID,), dtype=jnp.float32) * inv(D_IN), 'w2_w': _ternary(ks[3], (D_HID, D_IN)), 'w2_s': jax.random.uniform(ks[4], (D_HID,), dtype=jnp.float32) * inv(D_IN), 'h1_w': _ternary(ks[5], (D_HID, D_HID)), 'h1_s': jax.random.uniform(ks[6], (D_HID,), dtype=jnp.float32) * inv(D_HID), 'h2_w': _ternary(ks[7], (D_HID, D_HID)), 'h2_s': jax.random.uniform(ks[8], (D_HID,), dtype=jnp.float32) * inv(D_HID), 'w3_w': _ternary(ks[9], (D_IN, D_HID)), 'w3_s': jax.random.uniform(ks[10], (D_IN,), dtype=jnp.float32) * inv(D_HID)}
    _L1_ffn_in = _L1_ffn_setup()
    _d = {'L0_attn_x': _L0_attn_in['x'], 'L0_attn_W_in': _L0_attn_in['W_in'], 'L0_attn_dw_weight': _L0_attn_in['dw_weight'], 'L0_attn_dw_bias': _L0_attn_in['dw_bias'], 'L0_attn_W_bc': _L0_attn_in['W_bc'], 'L0_attn_W_out': _L0_attn_in['W_out'], 'L0_attn_skip': _L0_attn_in['skip'], 'L0_attn_A_log': _L0_attn_in['A_log'], 'L0_attn_dt_bias': _L0_attn_in['dt_bias'], 'L0_ffn_w1_w': _L0_ffn_in['w1_w'], 'L0_ffn_w1_s': _L0_ffn_in['w1_s'], 'L0_ffn_w2_w': _L0_ffn_in['w2_w'], 'L0_ffn_w2_s': _L0_ffn_in['w2_s'], 'L0_ffn_h1_w': _L0_ffn_in['h1_w'], 'L0_ffn_h1_s': _L0_ffn_in['h1_s'], 'L0_ffn_h2_w': _L0_ffn_in['h2_w'], 'L0_ffn_h2_s': _L0_ffn_in['h2_s'], 'L0_ffn_w3_w': _L0_ffn_in['w3_w'], 'L0_ffn_w3_s': _L0_ffn_in['w3_s'], 'L1_attn_norm_w': _L1_attn_in['norm_w'], 'L1_attn_Wq': _L1_attn_in['Wq'], 'L1_attn_Wkv': _L1_attn_in['Wkv'], 'L1_attn_Wout': _L1_attn_in['Wout'], 'L1_attn_Wg': _L1_attn_in['Wg'], 'L1_ffn_w1_w': _L1_ffn_in['w1_w'], 'L1_ffn_w1_s': _L1_ffn_in['w1_s'], 'L1_ffn_w2_w': _L1_ffn_in['w2_w'], 'L1_ffn_w2_s': _L1_ffn_in['w2_s'], 'L1_ffn_h1_w': _L1_ffn_in['h1_w'], 'L1_ffn_h1_s': _L1_ffn_in['h1_s'], 'L1_ffn_h2_w': _L1_ffn_in['h2_w'], 'L1_ffn_h2_s': _L1_ffn_in['h2_s'], 'L1_ffn_w3_w': _L1_ffn_in['w3_w'], 'L1_ffn_w3_s': _L1_ffn_in['w3_s']}
    _x0 = _d['L0_attn_x']
    _d['L0_attn_x'] = jax.random.normal(jax.random.fold_in(jax.random.key(seed), 1), (4, 512, 128), dtype=_x0.dtype)
    del _x0
    return _d

def reference(L0_attn_x, L0_attn_W_in, L0_attn_dw_weight, L0_attn_dw_bias, L0_attn_W_bc, L0_attn_W_out, L0_attn_skip, L0_attn_A_log, L0_attn_dt_bias, L0_ffn_w1_w, L0_ffn_w1_s, L0_ffn_w2_w, L0_ffn_w2_s, L0_ffn_h1_w, L0_ffn_h1_s, L0_ffn_h2_w, L0_ffn_h2_s, L0_ffn_w3_w, L0_ffn_w3_s, L1_attn_norm_w, L1_attn_Wq, L1_attn_Wkv, L1_attn_Wout, L1_attn_Wg, L1_ffn_w1_w, L1_ffn_w1_s, L1_ffn_w2_w, L1_ffn_w2_s, L1_ffn_h1_w, L1_ffn_h1_s, L1_ffn_h2_w, L1_ffn_h2_s, L1_ffn_w3_w, L1_ffn_w3_s):

    def _L0_attn_ref(x, W_in, dw_weight, dw_bias, W_bc, W_out, skip, A_log, dt_bias):
        import jax, jax.numpy as jnp
        import numpy as np
        B, T, D_MODEL = (2, 64, 128)
        D_INNER, D_HEAD, D_CONV = (256, 64, 4)
        N_HEADS, D_STATE = (32, 32)
        DT_MIN, DT_MAX, K_MAX, EPS = (0.0001, 0.1, 0.5, 1e-08)

        def _forward(x, W_in, dw_weight, dw_bias, W_bc, W_out, skip, A_log, dt_bias):
            Bsz, Tlen, D = x.shape
            DI, K = dw_weight.shape
            H, N = A_log.shape
            DH = DI // H
            proj = jnp.einsum('btd,od->bto', x, W_in)
            gate = proj[..., :DI]
            value_raw = proj[..., DI:2 * DI]
            params = proj[..., 2 * DI:].reshape(Bsz, Tlen, H, 2)
            xp = jnp.pad(value_raw, ((0, 0), (K - 1, 0), (0, 0)))
            conv = dw_bias + sum((xp[:, k:k + Tlen, :] * dw_weight[:, k] for k in range(K)))
            value = jax.nn.silu(conv)
            dt = jnp.clip(jax.nn.softplus(params[..., 0] + dt_bias), DT_MIN, DT_MAX)
            kd = K_MAX * jax.nn.sigmoid(params[..., 1])
            A = jnp.exp(A_log)
            bc = jnp.einsum('bti,oi->bto', value, W_bc).reshape(Bsz, Tlen, H, 4, N)
            bc = bc / (jnp.sqrt(jnp.sum(bc * bc, axis=-1, keepdims=True)) + EPS)
            Bz, Bx, Cz, Cx = (bc[..., 0, :], bc[..., 1, :], bc[..., 2, :], bc[..., 3, :])
            u = value.reshape(Bsz, Tlen, H, DH)

            def step(carry, inp):
                z, s = carry
                u_t, dt_t, k_t, Bz_t, Bx_t, Cz_t, Cx_t = inp
                dtE = dt_t[:, :, None, None]
                S = 1.0 / (1.0 + dt_t[..., None] * k_t[..., None] + (dt_t * dt_t)[..., None] * A)
                z = S[..., None] * (z - dtE * A[None, :, :, None] * s + dtE * (Bz_t[..., None] * u_t[:, :, None, :]))
                s = s + dtE * z + dtE * (Bx_t[..., None] * u_t[:, :, None, :])
                y = jnp.einsum('bhn,bhnd->bhd', Cz_t, z) + jnp.einsum('bhn,bhnd->bhd', Cx_t, s)
                return ((z, s), y)
            tm = lambda a: jnp.moveaxis(a, 1, 0)
            init = (jnp.zeros((Bsz, H, N, DH), x.dtype), jnp.zeros((Bsz, H, N, DH), x.dtype))
            _, ys = jax.lax.scan(step, init, (tm(u), tm(dt), tm(kd), tm(Bz), tm(Bx), tm(Cz), tm(Cx)))
            y = jnp.moveaxis(ys, 0, 1).reshape(Bsz, Tlen, DI)
            y = (y + skip * value) * jax.nn.silu(gate)
            return jnp.einsum('bti,oi->bto', y, W_out)
        return _forward(x, W_in, dw_weight, dw_bias, W_bc, W_out, skip, A_log, dt_bias)

    def _L0_ffn_ref(x, w1_w, w1_s, w2_w, w2_s, h1_w, h1_s, h2_w, h2_s, w3_w, w3_s):
        import jax, jax.numpy as jnp
        import numpy as np
        D_IN, D_HID = (128, 512)

        def _ternary(key, shape):
            return jax.random.randint(key, shape, -1, 2).astype(jnp.float32)

        def _tlin(x, w, s):
            return jnp.einsum('bsi,oi->bso', x, w) * s
        h = jax.nn.silu(_tlin(x, w1_w, w1_s)) * _tlin(x, w2_w, w2_s)
        h = jax.nn.gelu(_tlin(h, h1_w, h1_s), approximate=False)
        h = jax.nn.gelu(_tlin(h, h2_w, h2_s), approximate=False)
        return _tlin(h, w3_w, w3_s)

    def _L1_attn_ref(tokens, norm_w, Wq, Wkv, Wout, Wg):
        import jax, jax.numpy as jnp
        import numpy as np
        DIM = 128
        HEADS = 16
        DIM_HEAD = 64
        DIM_INNER = HEADS * DIM_HEAD
        SCALE = DIM_HEAD ** (-0.5)

        def rmsnorm(x, w):
            eps = jnp.asarray(jnp.finfo(x.dtype).eps, x.dtype)
            var = jnp.mean(jnp.square(x), axis=-1, keepdims=True)
            return x * jax.lax.rsqrt(var + eps) * w
        b, n, _ = tokens.shape
        x = rmsnorm(tokens, norm_w)
        q = x @ Wq
        kv = x @ Wkv
        k, v = jnp.split(kv, 2, axis=-1)

        def split_heads(t):
            return t.reshape(b, n, HEADS, DIM_HEAD).transpose(0, 2, 1, 3)
        q, k, v = map(split_heads, (q, k, v))
        sim = jnp.einsum('bhid,bhjd->bhij', q, k) * SCALE
        causal_mask = jnp.triu(jnp.ones((n, n), dtype=bool), k=1)
        sim = jnp.where(causal_mask, jnp.asarray(-jnp.finfo(sim.dtype).max, sim.dtype), sim)
        attn = jax.nn.softmax(sim, axis=-1)
        out = jnp.einsum('bhij,bhjd->bhid', attn, v)
        gates = jax.nn.sigmoid(x @ Wg)
        gates = gates.transpose(0, 2, 1)[..., None]
        out = gates * out
        out = out.transpose(0, 2, 1, 3).reshape(b, n, DIM_INNER)
        return out @ Wout

    def _L1_ffn_ref(x, w1_w, w1_s, w2_w, w2_s, h1_w, h1_s, h2_w, h2_s, w3_w, w3_s):
        import jax, jax.numpy as jnp
        import numpy as np
        D_IN, D_HID = (128, 512)

        def _ternary(key, shape):
            return jax.random.randint(key, shape, -1, 2).astype(jnp.float32)

        def _tlin(x, w, s):
            return jnp.einsum('bsi,oi->bso', x, w) * s
        h = jax.nn.silu(_tlin(x, w1_w, w1_s)) * _tlin(x, w2_w, w2_s)
        h = jax.nn.gelu(_tlin(h, h1_w, h1_s), approximate=False)
        h = jax.nn.gelu(_tlin(h, h2_w, h2_s), approximate=False)
        return _tlin(h, w3_w, w3_s)
    x = L0_attn_x
    x = x + _L0_attn_ref(_layernorm(x, axis=-1), L0_attn_W_in, L0_attn_dw_weight, L0_attn_dw_bias, L0_attn_W_bc, L0_attn_W_out, L0_attn_skip, L0_attn_A_log, L0_attn_dt_bias)
    x = x + _L0_ffn_ref(_layernorm(x, axis=-1), L0_ffn_w1_w, L0_ffn_w1_s, L0_ffn_w2_w, L0_ffn_w2_s, L0_ffn_h1_w, L0_ffn_h1_s, L0_ffn_h2_w, L0_ffn_h2_s, L0_ffn_w3_w, L0_ffn_w3_s)
    x = x + _L1_attn_ref(_layernorm(x, axis=-1), L1_attn_norm_w, L1_attn_Wq, L1_attn_Wkv, L1_attn_Wout, L1_attn_Wg)
    x = x + _L1_ffn_ref(_layernorm(x, axis=-1), L1_ffn_w1_w, L1_ffn_w1_s, L1_ffn_w2_w, L1_ffn_w2_s, L1_ffn_h1_w, L1_ffn_h1_s, L1_ffn_h2_w, L1_ffn_h2_s, L1_ffn_w3_w, L1_ffn_w3_s)
    return x

_drawn_inputs = setup_inputs


def setup_inputs(seed=0):
    import zlib

    import numpy as np

    out = dict(_drawn_inputs(seed))
    spreads = {'L0_attn_skip': (1.0, 0.2), 'L1_attn_norm_w': (1.0, 0.2)}
    factors = {}
    for name, (base, spread) in spreads.items():
        noise = np.random.default_rng([zlib.crc32(name.encode()), seed]).standard_normal(out[name].shape)
        drawn = base * np.exp(spread * noise) if base else spread * noise
        out[name] = jnp.asarray(drawn.astype(out[name].dtype))
    for name, factor in factors.items():
        out[name] = (out[name] * factor).astype(out[name].dtype)
    return out
```

```python
from contextlib import ExitStack

import concourse.bass as bass
from concourse import mybir

F32 = mybir.dt.float32
ACT = mybir.ActivationFunctionType
ALU = mybir.AluOpType
AX = mybir.AxisListType

P = 128
B, T, D = 4, 512, 128
TOK = B * T
TILES = TOK // P
TPB = T // P
DI, H, N, KC = 256, 32, 32, 4
DH = DI // H
G4 = 4
HG = H // G4
HN = G4 * N
REC = 5 * HN
STEPS = 16
HID = 512
HEADS, DHEAD = 16, 64
INNER = HEADS * DHEAD
DT_MIN, DT_MAX, K_MAX, NORM_EPS, LN_EPS = 1e-4, 0.1, 0.5, 1e-8, 1e-5
RMS_EPS = 1.1920928955078125e-07
MASKED = -1e30


class Kernel:

    def __init__(self, nc, ctx, debug):
        self.nc = nc
        self.debug = debug
        self.bank = [ctx.enter_context(nc.psum_tensor(f"bank{i}", [P, 512], F32)) for i in range(8)]
        self.x = ctx.enter_context(nc.sbuf_tensor("x", [P, TILES, D], F32))
        self.ident = ctx.enter_context(nc.sbuf_tensor("ident", [P, P], F32))


def tools(nc, ctx):
    sems = []

    def clear():
        if sems:
            nc.clear_and_free_semaphores(sems)
            nc.all_engine_barrier()

    ctx.callback(clear)

    def sb(name, *shape):
        return ctx.enter_context(nc.sbuf_tensor(name, list(shape), F32))

    def sem(name):
        sems.append(nc.alloc_semaphore(name))
        return sems[-1]

    return sb, sem


def load_and_identity(k, x_in):
    nc = k.nc
    with ExitStack() as ctx:
        sb, sem = tools(nc, ctx)
        x_loaded, cleared, ident_made = sem("x_loaded"), sem("id_cleared"), sem("ident_made")
        block = ctx.enter_context(nc.Block())

        @block.sync
        def _(sp):
            sp.dma_start(k.x[:], x_in.rearrange("(t p) d -> p t d", p=P)).then_inc(x_loaded, 16)
            sp.wait_ge(x_loaded, 16)

        @block.gpsimd
        def _(pool):
            pool.memset(k.ident[:], 0.0).then_inc(cleared, 1)
            pool.wait_ge(cleared, 1)
            pool.affine_select(out=k.ident[:], in_=k.ident[:], compare_op=ALU.not_equal, fill=1.0, base=0,
                               pattern=[[-1, P]], channel_multiplier=1).then_inc(ident_made, 1)


def wait_alone(eng, sem, value, passed):
    eng.wait_ge(sem, value)
    eng.sem_inc(passed)


def norm_transpose(k, xnT, tag, rms_weight=None):
    nc = k.nc
    with ExitStack() as ctx:
        sb, sem = tools(nc, ctx)
        stats = sb(f"stats{tag}", P, TILES, 6)
        mv = sb(f"mv{tag}", P, TILES, 2)
        std = sb(f"std{tag}", P, TILES)
        rstd = sb(f"rstd{tag}", P, TILES)
        xn = sb(f"xn{tag}", P, TILES, D)
        stats_made, mv_made, var_eps, std_made = (sem(f"{s}{tag}") for s in ("stats", "mv", "vare", "std"))
        rstd_made, xn_made, xnT_ready, xnT_taken = (sem(f"{s}{tag}") for s in ("rstd", "xn", "xnTr", "xnTt"))
        if rms_weight is not None:
            nw = sb(f"nw{tag}", P, 1)
            sq = sb(f"sq{tag}", P, 2, D)
            ms = sb(f"ms{tag}", P, TILES)
            rms = sb(f"rms{tag}", P, TILES)
            nw_loaded, sq_made, ms_eps, rms_std, rms_made, xr_made = (
                sem(f"{s}{tag}") for s in ("nwl", "sqm", "mse", "rmss", "rmsm", "xrm"))
        block = ctx.enter_context(nc.Block())

        @block.sync
        def _(sp):
            if rms_weight is not None:
                sp.dma_start(nw[:], rms_weight).then_inc(nw_loaded, 16)
                sp.wait_ge(nw_loaded, 16)

        @block.vector
        def _(dve):
            with dve.Fori(0, TILES) as t:
                dve.bn_stats(stats[:, t, :], k.x[:, t, :]).then_inc(stats_made, 1)
            dve.wait_ge(stats_made, TILES)
            for t in range(TILES):
                dve.bn_aggr(mv[:, t, :], stats[:, t, :]).then_inc(mv_made, 1)
            dve.wait_ge(mv_made, TILES)
            dve.tensor_scalar(std[:], mv[:, :, 1], LN_EPS, None, ALU.add).then_inc(var_eps, 1)
            dve.wait_ge(std_made, 1)
            dve.reciprocal(rstd[:], std[:]).then_inc(rstd_made, 1)
            dve.wait_ge(rstd_made, 1)
            for t in range(TILES):
                dve.tensor_scalar(xn[:, t, :], k.x[:, t, :], mv[:, t, 0:1], rstd[:, t:t + 1],
                                  ALU.subtract, ALU.mult).then_inc(xn_made, 1)
            if rms_weight is not None:
                dve.wait_ge(sq_made, TILES)
                dve.tensor_scalar(rms[:], ms[:], 1.0 / D, RMS_EPS, ALU.mult, ALU.add).then_inc(ms_eps, 1)
                dve.wait_ge(rms_std, 1)
                dve.reciprocal(rms[:], ms[:]).then_inc(rms_made, 1)
                dve.wait_ge(rms_made, 1)
                for t in range(TILES):
                    dve.tensor_scalar(xn[:, t, :], xn[:, t, :], rms[:, t:t + 1], None,
                                      ALU.mult).then_inc(xr_made, 1)

        @block.tensor
        def _(pe):
            for t in range(TILES):
                pe.wait_ge(xn_made if rms_weight is None else xr_made, t + 1)
                if t % 4 == 0 and t >= 8:
                    pe.wait_ge(xnT_taken, t // 4 - 1)
                pe.transpose(k.bank[t // 4 % 2][:, t % 4 * P:(t % 4 + 1) * P], xn[:, t, :],
                             k.ident[:]).then_inc(xnT_ready, 1)

        @block.scalar
        def _(act):
            act.wait_ge(var_eps, 1)
            act.activation(std[:], std[:], ACT.Sqrt).then_inc(std_made, 1)
            if rms_weight is not None:
                for t in range(TILES):
                    act.wait_ge(xn_made, t + 1)
                    if t >= 2:
                        act.wait_ge(sq_made, t - 1)
                    act.activation(sq[:, t % 2, :], xn[:, t, :], ACT.Square,
                                   accum_out=ms[:, t:t + 1]).then_inc(sq_made, 1)
                act.wait_ge(ms_eps, 1)
                act.activation(ms[:], rms[:], ACT.Sqrt).then_inc(rms_std, 1)
                act.wait_ge(nw_loaded, 16)
            for g in range(TILES // 4):
                act.wait_ge(xnT_ready, 4 * g + 4)
                scale = 1.0 if rms_weight is None else nw[:, 0:1]
                act.activation(xnT[:, g * 512:(g + 1) * 512], k.bank[g % 2][:], ACT.Copy,
                               scale=scale).then_inc(xnT_taken, 1)


def project(k, m, ins, scratch):
    nc = k.nc
    with ExitStack() as ctx:
        sb, sem = tools(nc, ctx)
        NW = DI + 2 * H
        w_in = sb("w_in", P, NW + DI)
        xnT = sb("xnT", P, TOK)
        raw = sb("raw_value", P, 2, B, T + KC - 1)
        conv = sb("conv", P, 2, TOK)
        par = sb("par", 2 * H, TOK)
        dw = sb("dw", P, 2, KC)
        db = sb("db", P, 2)
        dtb = sb("dtb", P, H)
        soft = sb("soft", P, 3, TILES * H)
        norm_transpose(k, xnT, "0")
        s = {n: sem("pj_" + n) for n in (
            "loaded", "ready", "taken", "padded", "conv", "value", "uT_ready", "uT_taken", "par_stored",
            "dt_biased", "abs", "exp", "ln", "relu", "sum", "clip")}
        block = ctx.enter_context(nc.Block())
        NJ = B + 2 * B + TILES

        @block.sync
        def _(sp):
            sp.dma_start(w_in[:], ins["w_in"]).then_inc(s["loaded"], 16)
            sp.dma_start(dw[:], ins["dw"].rearrange("(c p) k -> p c k", p=P)).then_inc(s["loaded"], 16)
            sp.dma_start(db[:], ins["db"]).then_inc(s["loaded"], 16)
            sp.dma_start(dtb[:], ins["dt_bias"].rearrange("(a h) -> a h", a=1).broadcast_to([P, H])).then_inc(s["loaded"], 16)
            sp.wait_ge(s["taken"], B)
            sp.dma_start(scratch["par"], par[:]).then_inc(s["par_stored"], 16)
            sp.wait_ge(s["par_stored"], 16)

        @block.tensor
        def _(pe):
            pe.wait_ge(s["loaded"], 64)
            for j in range(NJ):
                if j >= 4:
                    pe.wait_ge(s["taken"], j - 3)
                out = k.bank[j % 4]
                if j < B:
                    ins_ = pe.matmul(out[0:2 * H, :], w_in[:, DI:NW], xnT[:, j * T:(j + 1) * T])
                elif j < 3 * B:
                    c, b = divmod(j - B, B)
                    ins_ = pe.matmul(out[:], w_in[:, NW + c * P:NW + (c + 1) * P], xnT[:, b * T:(b + 1) * T])
                else:
                    t = j - 3 * B
                    ins_ = pe.matmul(out[:, 0:DI + H], xnT[:, t * P:(t + 1) * P], w_in[:, 0:DI + H])
                ins_.then_inc(s["ready"], 1)
            for g in range(TILES // 2):
                if g >= 4:
                    pe.wait_ge(s["uT_taken"], g - 3)
                for q in range(4):
                    t, c = 2 * g + q // 2, q % 2
                    pe.wait_ge(s["value"], (t // TPB) * 2 + c + 1)
                    ins_ = pe.transpose(k.bank[4 + g % 4][:, q * P:(q + 1) * P], m["valueT"][:, c, t * P:(t + 1) * P],
                                        k.ident[:])
                ins_.then_inc(s["uT_ready"], 1)

        @block.scalar
        def _(act):
            for j in range(NJ):
                act.wait_ge(s["ready"], j + 1)
                src = k.bank[j % 4]
                if j < B:
                    act.copy(par[:, j * T:(j + 1) * T], src[0:2 * H, :]).then_inc(s["taken"], 1)
                elif j < 3 * B:
                    c, b = divmod(j - B, B)
                    act.copy(raw[:, c, b, KC - 1:], src[:]).then_inc(s["taken"], 1)
                else:
                    t = j - 3 * B
                    act.copy(m["dt"][:, t, :], src[:, DI:DI + H])
                    act.activation(m["gate"][:, t, :], src[:, 0:DI], ACT.Silu).then_inc(s["taken"], 1)
            for n in range(2 * B):
                b, c = divmod(n, 2)
                act.wait_ge(s["conv"], KC * (n + 1))
                act.activation(m["valueT"][:, c, b * T:(b + 1) * T], conv[:, c, b * T:(b + 1) * T],
                               ACT.Silu).then_inc(s["value"], 1)
            for g in range(TILES // 2):
                act.wait_ge(s["uT_ready"], g + 1)
                act.copy(m["u"][:, 2 * g:2 * g + 2, :].rearrange("p t c -> p (t c)"),
                         k.bank[4 + g % 4][:]).then_inc(s["uT_taken"], 1)
            act.wait_ge(s["dt_biased"], 1)
            act.activation(soft[:, 1, :], soft[:, 0, :], ACT.Abs).then_inc(s["abs"], 1)
            act.wait_ge(s["abs"], 1)
            act.activation(soft[:, 1, :], soft[:, 1, :], ACT.Exp, scale=-1.0).then_inc(s["exp"], 1)
            act.wait_ge(s["exp"], 1)
            act.activation(soft[:, 2, :], soft[:, 1, :], ACT.Ln, bias=1.0).then_inc(s["ln"], 1)

        @block.vector
        def _(dve):
            dve.memset(raw[:, :, :, 0:KC - 1], 0.0).then_inc(s["padded"], 1)
            dve.wait_ge(s["padded"], 1)
            dve.wait_ge(s["loaded"], 64)
            for n in range(2 * B):
                b, c = divmod(n, 2)
                dve.wait_ge(s["taken"], B + c * B + b + 1)
                acc = conv[:, c, b * T:(b + 1) * T]
                dve.tensor_scalar(acc, raw[:, c, b, 0:T], dw[:, c, 0:1], db[:, c:c + 1], ALU.mult,
                                  ALU.add).then_inc(s["conv"], 1)
                for tap in range(1, KC):
                    dve.wait_ge(s["conv"], KC * n + tap)
                    dve.scalar_tensor_tensor(out=acc, in0=raw[:, c, b, tap:tap + T], scalar=dw[:, c, tap:tap + 1],
                                             in1=acc, op0=ALU.mult, op1=ALU.add).then_inc(s["conv"], 1)
            dve.wait_ge(s["taken"], NJ)
            v = soft[:, 0, :].rearrange("p (t h) -> p t h", h=H)
            dve.tensor_tensor(v, m["dt"][:], dtb[:].unsqueeze(1).broadcast_to([P, TILES, H]),
                              ALU.add).then_inc(s["dt_biased"], 1)
            dve.wait_ge(s["ln"], 1)
            dve.tensor_scalar(soft[:, 1, :], soft[:, 0, :], 0.0, None, ALU.max).then_inc(s["relu"], 1)
            dve.wait_ge(s["relu"], 1)
            dve.tensor_tensor(soft[:, 1, :], soft[:, 1, :], soft[:, 2, :], ALU.add).then_inc(s["sum"], 1)
            dve.wait_ge(s["sum"], 1)
            dve.tensor_scalar(m["dt"][:].rearrange("p t h -> p (t h)"), soft[:, 1, :], DT_MIN, DT_MAX, ALU.max,
                              ALU.min).then_inc(s["clip"], 1)


def recur(k, m, ins, scratch):
    nc = k.nc
    with ExitStack() as ctx:
        sb, sem = tools(nc, ctx)
        SLOTS = 2 * STEPS
        X = sb("X", P, SLOTS, REC)
        praw = sb("praw", P, 2, G4, P)
        coef = sb("coef", P, 4, G4, P)
        tmp = sb("ctmp", P, 3, G4 * P)
        A = sb("A", P, HN)
        dtb = sb("dtb2", P, G4)
        a = sb("a", P, 2, STEPS, HN)
        g = sb("g", P, 2, STEPS + 1, HN)
        d0 = sb("d0", P, STEPS, HN)
        t1 = sb("t1", P, 2 * HN)
        t23 = sb("t23", P, 4 * HN)
        phi = sb("phi_rows", P, 2, 2, P)
        s = {n: sem("rc_" + n) for n in (
            "pool_passed", "sp_passed", "loaded", "prep", "aexp", "start", "id_stored", "a_ready", "a_used", "rec", "g1", "g_ready", "gch", "ln",
            "d0", "n1", "n2", "det", "phi", "phiT", "phi_copied", "phi_done", "sigm")}
        stored = [sem(f"rc_stored{h}") for h in range(2)]
        block = ctx.enter_context(nc.Block())
        coef_r = coef[:].rearrange("p c h t -> p (c h) t")

        @block.sync
        def _(sp):
            n = 0
            for hg in range(HG):
                lanes = slice(hg * TILES, (hg + 1) * TILES)
                for kind in range(2):
                    src = scratch["par"][kind * H + hg * G4:kind * H + (hg + 1) * G4, :]
                    sp.dma_start(praw[lanes, kind], src.rearrange("h (c t) -> c h t", t=P)).then_inc(s["loaded"], 16)
                al = ins["A_log"][hg * G4:(hg + 1) * G4, :].rearrange("h n -> (h n)").unsqueeze(0)
                sp.dma_start(A[lanes, :], al.broadcast_to([TILES, HN])).then_inc(s["loaded"], 16)
                bl = ins["dt_bias"][hg * G4:(hg + 1) * G4].unsqueeze(0)
                sp.dma_start(dtb[lanes, :], bl.broadcast_to([TILES, G4])).then_inc(s["loaded"], 16)
                n += 4
            for h in range(2):
                sp.sem_inc(stored[h], 16)
            sp.wait_ge(s["start"], 2)
            sp.dma_start(scratch["psi"][:, 0, 0:4 * HN], X[:, SLOTS - 1, 0:4 * HN]).then_inc(s["id_stored"], 16)
            with sp.Fori(0, P // SLOTS) as i:
                for h in range(2):
                    wait_alone(sp, s["rec"], SLOTS * 4 * i + (h + 1) * STEPS * 4 + 1, s["sp_passed"])
                    wait_alone(sp, s["det"], 2 * i + h + 2, s["sp_passed"])
                    sp.dma_start(scratch["psi"][:, bass.ds(1 + SLOTS * i + h * STEPS, STEPS), :],
                                 X[:, h * STEPS:(h + 1) * STEPS, :]).then_inc(stored[h], 16)
            for h in range(2):
                sp.wait_ge(stored[h], 16 * (P // SLOTS) + 16)
            sp.wait_ge(s["id_stored"], 16)

        LOADED = 16 * 4 * HG

        @block.scalar
        def _(act):
            act.wait_ge(s["loaded"], LOADED)
            act.activation(A[:], A[:], ACT.Exp).then_inc(s["aexp"], 1)
            act.wait_ge(s["prep"], 1)
            act.activation(tmp[:, 1, :], tmp[:, 0, :], ACT.Abs).then_inc(s["sigm"], 1)
            act.wait_ge(s["sigm"], 1)
            act.activation(tmp[:, 1, :], tmp[:, 1, :], ACT.Exp, scale=-1.0).then_inc(s["sigm"], 1)
            act.wait_ge(s["sigm"], 2)
            act.activation(tmp[:, 1, :], tmp[:, 1, :], ACT.Ln, bias=1.0).then_inc(s["sigm"], 1)
            act.activation(tmp[:, 2, :], praw[:, 1].rearrange("p h t -> p (h t)"), ACT.Exp,
                           scale=-1.0).then_inc(s["sigm"], 1)
            with act.Fori(0, P // SLOTS) as i:
                for h in range(2):
                    act.wait_ge(s["g_ready"], (2 * i + h + 1) * STEPS)
                    act.wait_ge(s["det"], 2 * i + h + 1)
                    act.activation(d0[:], g[:, h, 1:], ACT.Ln).then_inc(s["ln"], 1)
                    act.wait_ge(s["ln"], 2 * i + h + 1)
                    act.activation(d0[:], d0[:], ACT.Exp, scale=-1.0).then_inc(s["d0"], 1)

        @block.vector
        def _(dve):
            rec = s["rec"]
            dve.sem_inc(rec, 1)
            dve.memset(X[:, SLOTS - 1, 0:4 * HN], 0.0).then_inc(s["start"], 1)
            dve.wait_ge(s["start"], 1)
            ends = X[:, SLOTS - 1, 0:4 * HN].rearrange("p (c n) -> p c n", n=HN)[:, 0:4:3, :]
            dve.memset(ends, 1.0).then_inc(s["start"], 1)
            dve.wait_ge(s["loaded"], LOADED)
            v = tmp[:, 0, :].rearrange("p (h t) -> p h t", t=P)
            dve.tensor_tensor(v, praw[:, 0], dtb[:].unsqueeze(2).broadcast_to([P, G4, P]), ALU.add).then_inc(s["prep"], 1)
            dve.wait_ge(s["sigm"], 4)
            dve.wait_ge(s["prep"], 1)
            dve.tensor_scalar(tmp[:, 0, :], tmp[:, 0, :], 0.0, None, ALU.max).then_inc(s["prep"], 1)
            dve.wait_ge(s["prep"], 2)
            dve.tensor_tensor(tmp[:, 0, :], tmp[:, 0, :], tmp[:, 1, :], ALU.add).then_inc(s["prep"], 1)
            dve.wait_ge(s["prep"], 3)
            dve.tensor_scalar(coef[:, 0].rearrange("p h t -> p (h t)"), tmp[:, 0, :], DT_MIN, DT_MAX, ALU.max,
                              ALU.min).then_inc(s["prep"], 1)
            dve.tensor_scalar(tmp[:, 2, :], tmp[:, 2, :], 1.0, None, ALU.add).then_inc(s["prep"], 1)
            dve.wait_ge(s["prep"], 5)
            dve.reciprocal(tmp[:, 1, :], tmp[:, 2, :]).then_inc(s["prep"], 1)
            dve.tensor_copy(coef[:, 1], coef[:, 0]).then_inc(s["prep"], 1)
            dve.wait_ge(s["prep"], 7)
            dve.scalar_tensor_tensor(out=tmp[:, 0, :], in0=tmp[:, 1, :], scalar=K_MAX,
                                     in1=coef[:, 0].rearrange("p h t -> p (h t)"), op0=ALU.mult,
                                     op1=ALU.mult).then_inc(s["prep"], 1)
            dve.wait_ge(s["prep"], 8)
            for c in (2, 3):
                dve.tensor_scalar(coef[:, c].rearrange("p h t -> p (h t)"), tmp[:, 0, :], 1.0, None,
                                  ALU.add).then_inc(s["prep"], 1)
            dve.wait_ge(s["prep"], 10)
            dve.wait_ge(s["id_stored"], 16)
            with dve.Fori(0, P // SLOTS) as i:
                for j in range(SLOTS):
                    h, q = divmod(j, STEPS)
                    if q == 0:
                        dve.wait_ge(s["a_ready"], 2 * i + h + 1)
                        dve.wait_ge(stored[h], 16 * i + 16)
                    last = X[:, (j - 1) % SLOTS]
                    now = X[:, j]
                    n0 = SLOTS * 4 * i + 4 * j + 1
                    dve.wait_ge(rec, n0)
                    dve.tensor_tensor(t1[:].rearrange("p (c n) -> p c n", c=2),
                                      a[:, h, q].unsqueeze(1).broadcast_to([P, 2, HN]),
                                      last[:, 2 * HN:4 * HN].rearrange("p (c n) -> p c n", c=2),
                                      ALU.mult).then_inc(rec, 1)
                    ct = coef_r[:, :, bass.ds(SLOTS * i + j, 1)].broadcast_to([P, 4 * G4, N])
                    dve.tensor_tensor(t23[:].rearrange("p (c n) -> p c n", n=N), ct,
                                      last[:, 0:4 * HN].rearrange("p (c n) -> p c n", n=N), ALU.mult).then_inc(rec, 1)
                    dve.wait_ge(rec, n0 + 1)
                    dve.tensor_tensor(now[:, 0:2 * HN], last[:, 0:2 * HN], t1[:], ALU.subtract).then_inc(rec, 1)
                    dve.wait_ge(rec, n0 + 2)
                    ins_ = dve.tensor_tensor(now[:, 2 * HN:4 * HN], t23[:, 0:2 * HN], t23[:, 2 * HN:4 * HN], ALU.add)
                    ins_.then_inc(rec, 1)
            dve.wait_ge(s["det"], 2 * (P // SLOTS) + 1)
            dve.wait_ge(rec, 4 * P + 1)
            end = X[:, SLOTS - 1]
            for row in range(2):
                for pair in range(2):
                    e = end[:, 2 * row * HN:(2 * row + 2) * HN].rearrange("p (c q h n) -> p q h c n", c=2, q=2, h=2)
                    dd = end[:, 4 * HN:5 * HN].rearrange("p (q h n) -> p q h n", q=2, h=2)[:, pair]
                    dve.tensor_tensor(phi[:, pair, row].rearrange("p (h c n) -> p h c n", h=2, c=2), e[:, pair],
                                      dd.unsqueeze(2).broadcast_to([P, 2, 2, N]), ALU.mult).then_inc(s["phi"], 1)
            ent = m["enter"]
            dve.memset(ent[:], 0.0).then_inc(s["phi_done"], 1)
            dve.wait_ge(s["phi_done"], 1)
            dve.wait_ge(s["phiT"], 4)
            dst = ent[:].rearrange("p q g (b c) -> p q g b c", c=TPB)
            srcT = k.bank[0][:].rearrange("p (q g b c) -> p q g b c", q=4, g=HG, b=B)
            for q in range(4):
                for b in range(B):
                    dve.tensor_copy(dst[:, q, :, b, 1:TPB], srcT[:, q, :, b, 0:TPB - 1]).then_inc(s["phi_done"], 1)

        @block.tensor
        def _(pe):
            for q in range(4):
                pe.wait_ge(s["phi"], 4)
                pe.transpose(k.bank[0][:, q * P:(q + 1) * P], phi[:, q // 2, q % 2, :], k.ident[:]).then_inc(s["phiT"], 1)

        @block.gpsimd
        def _(pool):
            pool.sem_inc(s["det"], 1)
            pool.memset(g[:, 1, STEPS], 1.0).then_inc(s["g1"], 1)
            pool.wait_ge(s["prep"], 10)
            pool.wait_ge(s["aexp"], 1)
            pool.wait_ge(s["g1"], 1)
            with pool.Fori(0, P // SLOTS) as i:
                for h in range(2):
                    blk = 2 * i + h
                    dt = coef[:, 0, :, bass.ds(SLOTS * i + h * STEPS, STEPS)].rearrange("p h t -> p t h")
                    f = coef[:, 2, :, bass.ds(SLOTS * i + h * STEPS, STEPS)].rearrange("p h t -> p t h")
                    dt = dt.unsqueeze(3).broadcast_to([P, STEPS, G4, N])
                    f = f.unsqueeze(3).broadcast_to([P, STEPS, G4, N])
                    Ab = A[:].rearrange("p (h n) -> p h n", n=N).unsqueeze(1).broadcast_to([P, STEPS, G4, N])
                    ah = a[:, h].rearrange("p t (h n) -> p t h n", n=N)
                    gh = g[:, h, 1:].rearrange("p t (h n) -> p t h n", n=N)
                    wait_alone(pool, s["rec"], SLOTS * 4 * i + 1, s["pool_passed"])
                    pool.tensor_tensor(ah, dt, Ab, ALU.mult).then_inc(s["a_ready"], 1)
                    pool.wait_ge(s["a_ready"], blk + 1)
                    wait_alone(pool, s["det"], blk + 1, s["pool_passed"])
                    pool.tensor_tensor(gh, dt, ah, ALU.mult).then_inc(s["g1"], 1)
                    wait_alone(pool, s["g1"], 2 * blk + 2, s["pool_passed"])
                    pool.tensor_tensor(gh, gh, f, ALU.add).then_inc(s["g1"], 1)
                    pool.wait_ge(s["g1"], 2 * blk + 3)
                    for q in range(STEPS):
                        before = g[:, 1 - h, STEPS] if q == 0 else g[:, h, q]
                        pool.tensor_tensor(g[:, h, q + 1], g[:, h, q + 1], before, ALU.mult).then_inc(s["g_ready"], 1)
                        pool.wait_ge(s["g_ready"], STEPS * blk + q + 1)
                    pool.wait_ge(s["d0"], blk + 1)
                    wait_alone(pool, stored[h], 16 * i + 16, s["pool_passed"])
                    dd = X[:, h * STEPS:(h + 1) * STEPS, 4 * HN:5 * HN]
                    pool.tensor_tensor(dd, g[:, h, 1:], d0[:], ALU.mult).then_inc(s["n1"], 1)
                    wait_alone(pool, s["n1"], blk + 1, s["pool_passed"])
                    pool.tensor_scalar(dd, dd, -1.0, 2.0, ALU.mult, ALU.add).then_inc(s["n2"], 1)
                    pool.wait_ge(s["n2"], blk + 1)
                    pool.tensor_tensor(dd, dd, d0[:], ALU.mult).then_inc(s["det"], 1)
                    pool.wait_ge(s["det"], blk + 2)


def mix(k, m, ins, scratch):
    nc = k.nc
    BODY = 2 * HG
    LOOPS = TILES // 2
    RING = 4
    with ExitStack() as ctx:
        sb, sem = tools(nc, ctx)
        w_bc = sb("w_bc", P, 2, 4 * N * H)
        vt = sb("vt", P, 2, 2, P)
        pt = sb("pt", P, 2, HG, REC)
        ps = sb("ps", P, 2, HG, 2 * HN)
        sq = sb("sq", P, 2, 4 * HN)
        ss = sb("ss", P, 2, 4 * G4)
        nr = sb("nr", P, 2, 4 * G4)
        rn = sb("rn", P, 4 * G4)
        sc = sb("sc", P, 4, HN)
        cd = sb("cd", P, 2, HN)
        pp = sb("pp", P, 2, 2, HN)
        qq = sb("qq", P, 4, HN)
        cb = sb("cb", P, 4, 2, G4, 2 * N)
        qk = sb("qk", P, 4, 2, 2, P)
        pm = sb("pm", P, 2, 2, 2, P)
        gs = sb("gs", P, 2 * HG, 2, DH)
        tk = sb("tk", P, 2, 2 * HG, 2 * DH)
        hst = sb("hst", P, 2 * HG, 2, DH)
        route = sb("route", P, 2, 2, 2, N)
        s = {n: sem("mx_" + n) for n in (
            "w_loaded", "staged", "bc_ready", "bc_squared", "reduced", "rooted", "rn", "bc_scaled", "cd", "pp", "q1",
            "q2", "ct", "cb_ready", "tp_ready", "qk_copied", "g_ready", "s_ready", "s_copied", "masked", "y_unit",
            "y_copied", "gs", "state_ready", "r_ready", "h_ready", "init", "pool_passed")}
        t_loaded = [sem(f"mx_tl{h}") for h in range(2)]
        BC, TP, SE, SO, YB, GB = k.bank[0:2], k.bank[2:4], k.bank[4], k.bank[5], k.bank[6], k.bank[7]
        block = ctx.enter_context(nc.Block())

        def run(eng, step, first, most):
            for n in range(first, 0):
                step(0, n, 0, BODY)
            with eng.Fori(0, LOOPS - 1) as i:
                for n in range(BODY):
                    step(i, n, 0, BODY + most)
            for n in range(BODY):
                step(LOOPS - 1, n, 0, BODY)

        psi = scratch["psi"].rearrange("(g c) t f -> c t g f", g=HG)

        @block.sync
        def _(sp):
            sp.dma_start(w_bc[:], ins["w_bc"].rearrange("(c p) o -> p c o", p=P)).then_inc(s["w_loaded"], 16)

            def load(t, h):
                sp.dma_start(pt[:, h], psi[t, 1:P + 1]).then_inc(t_loaded[h], 16)
                sp.dma_start(ps[:, h], psi[t, 0:P, :, 2 * HN:4 * HN]).then_inc(t_loaded[h], 16)

            load(0, 0)
            load(1, 1)
            with sp.Fori(0, LOOPS - 1) as i:
                for h in range(2):
                    sp.wait_ge(s["cb_ready"], BODY * i + HG * (h + 1))
                    sp.dma_start(pt[:, h], psi[bass.ds(2 * i + 2 + h, 1), 1:P + 1].rearrange("c t g f -> (c t) g f")
                                 ).then_inc(t_loaded[h], 16)
                    sp.dma_start(ps[:, h], psi[bass.ds(2 * i + 2 + h, 1), 0:P, :, 2 * HN:4 * HN].rearrange(
                        "c t g f -> (c t) g f")).then_inc(t_loaded[h], 16)

        @block.tensor
        def _(pe):
            def tile_slice(ap, i, n, lo, w):
                return ap[:, 2 * i + n // HG, lo:lo + w]

            def step(i, n, lo, hi):
                unit = BODY * i
                if lo <= n < hi and n < BODY:
                    hg = n % HG
                    pe.wait_ge(s["masked"], unit + n + 1)
                    if hg == 0:
                        pe.wait_ge(s["h_ready"], 2 * (2 * i + n // HG) + 3)
                    for pair in range(2):
                        c0 = (2 * hg + pair) * 2 * DH
                        pe.matmul(YB[:, c0:c0 + 2 * DH], qk[:, n % 4, 0, pair], hst[:, 2 * hg + pair],
                                  start=True, stop=False)
                        for h in range(2):
                            y = pe.matmul(YB[:, c0 + h * DH:c0 + (h + 1) * DH], pm[:, n % 2, h, pair],
                                          tile_slice(m["u"], i, n, c0 + h * DH, DH), start=False, stop=(h == 1))
                    y.then_inc(s["y_unit"], 1)
                if lo <= n + 3 < hi:
                    q = n + 3
                    if not (isinstance(i, int) and i == 0 and q < 2):
                        pe.wait_ge(s["bc_squared"], unit + q - 1)
                        pe.wait_ge(s["bc_scaled"], unit + q - 1)
                    if q % HG == 0:
                        pe.wait_ge(s["staged"], 2 * i + q // HG + 1)
                    for c in range(2):
                        mm = pe.matmul(BC[q % 2][:], vt[:, q // HG % 2, c], w_bc[:, c, q % HG * 4 * HN:(q % HG + 1) * 4 * HN],
                                       start=(c == 0), stop=(c == 1))
                    mm.then_inc(s["bc_ready"], 1)
                if lo <= n + 1 < hi:
                    q = n + 1
                    pe.wait_ge(s["qk_copied"], unit + q + 1)
                    if not (isinstance(i, int) and i == 0 and q < 1):
                        pe.wait_ge(s["s_copied"], 2 * (unit + q))
                    for pair in range(2):
                        for h in range(2):
                            lane = slice(64 * h, 64 * h + 64)
                            mm = pe.matmul((SE, SO)[h][:, pair * P:(pair + 1) * P], qk[lane, q % 4, 1, pair],
                                           qk[lane, q % 4, 0, pair])
                    mm.then_inc(s["s_ready"], 1)
                if lo <= n + 2 < hi:
                    q = n + 2
                    pe.wait_ge(s["cb_ready"], unit + q + 1)
                    if not (isinstance(i, int) and i == 0 and q < 2):
                        pe.wait_ge(s["qk_copied"], unit + q - 1)
                    for which in range(2):
                        for pair in range(2):
                            c0 = (2 * which + pair) * P
                            mm = pe.transpose(TP[q % 2][:, c0:c0 + P],
                                              cb[:, q % 4, which, 2 * pair:2 * pair + 2].rearrange("p h n -> p (h n)"),
                                              k.ident[:])
                    mm.then_inc(s["tp_ready"], 1)
                if lo <= n + 1 < hi:
                    q = n + 1
                    if q % HG == 0:
                        pe.wait_ge(s["gs"], 2 * i + q // HG + 1)
                    for pair in range(2):
                        c0 = (2 * (q % HG) + pair) * 2 * DH
                        mm = pe.matmul(GB[:, c0:c0 + 2 * DH],
                                       cb[:, q % 4, 1, 2 * pair:2 * pair + 2].rearrange("p h n -> p (h n)"),
                                       tile_slice(m["u"], i, q, c0, 2 * DH))
                    mm.then_inc(s["g_ready"], 1)
                if lo <= n + 1 < hi and (n + 1) % HG == 0:
                    t = 2 * i + (n + 1) // HG
                    pe.wait_ge(s["state_ready"], t + 1)
                    if not isinstance(t, int) or t > 0:
                        pe.wait_ge(s["y_copied"], t)
                    for r in range(2):
                        mm = pe.matmul(YB[:, 256:512], route[:, r].rearrange("p h r n -> p (h r n)"),
                                       tk[:, r].rearrange("p g d -> p (g d)"), start=(r == 0), stop=(r == 1))
                    mm.then_inc(s["r_ready"], 1)

            for name in ("tp_ready", "g_ready", "y_unit"):
                pe.sem_inc(s[name], RING)
            pe.wait_ge(s["w_loaded"], 16)
            run(pe, step, -3, 3)

        @block.scalar
        def _(act):
            def step(i, n, lo, hi):
                unit = BODY * i
                if lo <= n + 3 < hi:
                    q = n + 3
                    act.wait_ge(s["bc_ready"], unit + q + 1)
                    if not (isinstance(i, int) and i == 0 and q < 2):
                        act.wait_ge(s["reduced"], unit + q - 1)
                    act.activation(sq[:, q % 2], BC[q % 2][:], ACT.Square).then_inc(s["bc_squared"], 1)
                if lo <= n + 1 < hi:
                    q = n + 1
                    act.wait_ge(s["s_ready"], unit + q + 1)
                    act.wait_ge(s["y_unit"], unit + q + RING - 1)
                    for h in range(2):
                        act.copy(pm[:, q % 2, h].rearrange("p a t -> p (a t)"), (SE, SO)[h][:, 0:2 * P]
                                 ).then_inc(s["s_copied"], 1)
                if lo <= n + 3 < hi:
                    q = n + 3
                    act.wait_ge(s["reduced"], unit + q + 1)
                    if not (isinstance(i, int) and i == 0 and q < 2):
                        act.wait_ge(s["rn"], 3 * (unit + q - 2) + 1)
                    act.activation(nr[:, q % 2], ss[:, q % 2], ACT.Sqrt).then_inc(s["rooted"], 1)
                if lo <= n + 2 < hi:
                    q = n + 2
                    act.wait_ge(s["tp_ready"], unit + q + 1 + RING)
                    act.wait_ge(s["y_unit"], unit + q + 1)
                    act.copy(qk[:, q % 4].rearrange("p a b t -> p (a b t)"), TP[q % 2][:]).then_inc(s["qk_copied"], 1)
                if lo <= n < hi and n < BODY and n % HG == HG - 1:
                    t = 2 * i + n // HG
                    act.wait_ge(s["y_unit"], unit + n + 1 + RING)
                    act.copy(m["y"][:, t, :], YB[:, 0:DI]).then_inc(s["y_copied"], 1)
                if lo <= n + 1 < hi and (n + 1) % HG == 0:
                    t = 2 * i + (n + 1) // HG
                    act.wait_ge(s["r_ready"], t + 1)
                    act.wait_ge(s["gs"], t + 1)
                    for h in range(2):
                        lane = slice(64 * h, 64 * h + 64)
                        act.copy(hst[lane, :, h, :], YB[lane, 256:512].rearrange("p (g h d) -> p g h d", h=2, d=DH)[:, :, h]
                                 ).then_inc(s["h_ready"], 1)

            act.wait_ge(s["init"], 2)
            act.sem_inc(s["h_ready"], 1)
            run(act, step, -3, 3)

        @block.vector
        def _(dve):
            dve.memset(hst[:], 0.0).then_inc(s["init"], 1)
            dve.memset(GB[:, 0:256], 0.0).then_inc(s["init"], 1)
            dve.memset(route[:], 0.0).then_inc(s["init"], 1)
            dve.wait_ge(s["init"], 3)
            idr = k.ident[:].rearrange("p (h c n) -> p h c n", h=2, c=2)
            for r in range(2):
                dve.tensor_tensor(route[:, r, :, r, :], idr[:, :, 0, :], idr[:, :, 1, :], ALU.add).then_inc(s["init"], 1)
            dve.wait_ge(s["init"], 5)

            def reduce(i, q):
                unit = BODY * i
                dve.wait_ge(s["bc_squared"], unit + q + 1)
                if not (isinstance(i, int) and i == 0 and q < 2):
                    dve.wait_ge(s["rooted"], unit + q - 1)
                dve.tensor_reduce(ss[:, q % 2], sq[:, q % 2].rearrange("p (a n) -> p a n", n=N), AX.X,
                                  ALU.add).then_inc(s["reduced"], 1)

            def step(i, n, lo, hi):
                u = BODY * i + n
                h, hg = n // HG % 2, n % HG
                if n >= 0:
                    dve.wait_ge(s["rooted"], u + 1)
                    dve.tensor_scalar(nr[:, n % 2], nr[:, n % 2], NORM_EPS, None, ALU.add).then_inc(s["rn"], 1)
                    dve.wait_ge(s["rn"], 3 * u + 1)
                    dve.reciprocal(rn[:], nr[:, n % 2]).then_inc(s["rn"], 1)
                    dve.wait_ge(s["rn"], 3 * u + 2)
                    rb = rn[:].rearrange("p (h c) -> p h c", c=4)
                    dt = m["dt"][:, 2 * i + n // HG, hg * G4:(hg + 1) * G4].unsqueeze(2).broadcast_to([P, G4, 2])
                    dve.tensor_tensor(rb[:, :, 0:2], rb[:, :, 0:2], dt, ALU.mult).then_inc(s["rn"], 1)
                    dve.wait_ge(s["bc_ready"], u + 1)
                    dve.wait_ge(s["rn"], 3 * u + 3)
                    dve.tensor_tensor(sc[:].rearrange("p c (h n) -> p h c n", n=N),
                                      BC[n % 2][:].rearrange("p (h c n) -> p h c n", c=4, n=N),
                                      rb.unsqueeze(3).broadcast_to([P, G4, 4, N]), ALU.mult).then_inc(s["bc_scaled"], 1)
                if lo <= n + 1 < hi:
                    reduce(i, n + 1)
                if n < 0:
                    return
                if hg == 0:
                    dve.wait_ge(t_loaded[h], 32 * i + 32)
                dve.wait_ge(s["bc_scaled"], u + 1)
                z = pt[:, h, hg, :]
                dve.tensor_tensor(cd[:], sc[:, 2:4], z[:, 4 * HN:].unsqueeze(1).broadcast_to([P, 2, HN]),
                                  ALU.mult).then_inc(s["cd"], 1)
                dve.tensor_tensor(qq[:, 0:2], sc[:, 0:1].broadcast_to([P, 2, HN]),
                                  ps[:, h, hg].rearrange("p (c n) -> p c n", n=HN), ALU.mult).then_inc(s["q1"], 1)
                dve.wait_ge(s["cd"], u + 1)
                dve.tensor_tensor(pp[:], cd[:].unsqueeze(2).broadcast_to([P, 2, 2, HN]),
                                  z[:, 0:4 * HN].rearrange("p (r c n) -> p r c n", r=2, c=2), ALU.mult).then_inc(s["pp"], 1)
                dve.tensor_tensor(qq[:, 2:4], sc[:, 1:2].broadcast_to([P, 2, HN]),
                                  z[:, 0:2 * HN].rearrange("p (c n) -> p c n", n=HN), ALU.mult).then_inc(s["q2"], 1)
                dve.wait_ge(s["pp"], u + 1)
                dve.wait_ge(s["tp_ready"], u + 1)
                dve.wait_ge(s["g_ready"], u + 1)
                dve.tensor_tensor(cb[:, n % 4, 0].rearrange("p h (c n) -> p c h n", c=2),
                                  pp[:, 0].rearrange("p c (h n) -> p c h n", n=N),
                                  pp[:, 1].rearrange("p c (h n) -> p c h n", n=N), ALU.add).then_inc(s["ct"], 1)
                dve.wait_ge(s["q2"], u + 1)
                dst = cb[:, n % 4, 1].rearrange("p h (c n) -> p c h n", c=2)
                qv = qq[:].rearrange("p c (h n) -> p c h n", n=N)
                dve.tensor_tensor(dst[:, 0], qv[:, 1], qv[:, 3], ALU.subtract).then_inc(s["ct"], 1)
                dve.wait_ge(s["ct"], 2 * u + 2)
                dve.tensor_tensor(dst[:, 1], qv[:, 2], qv[:, 0], ALU.subtract).then_inc(s["cb_ready"], 1)
                dve.wait_ge(s["cb_ready"], u + 1)
                if hg == 1:
                    t = 2 * i + n // HG
                    dve.wait_ge(s["g_ready"], HG * t + RING)
                    dve.wait_ge(s["h_ready"], 2 * t + 1)
                    dve.tensor_tensor(gs[:].rearrange("p g h d -> p (g h d)"), hst[:].rearrange("p g h d -> p (g h d)"),
                                      GB[:, 0:256], ALU.add).then_inc(s["gs"], 1)
                    dve.wait_ge(s["gs"], t + 1)
                    for r in range(2):
                        e = m["enter"][:].rearrange("p (q r) g t -> p r g q t", r=2)[:, r, :, :, t]
                        ins_ = dve.tensor_tensor(
                            tk[:, r].rearrange("p (g q) d -> p g q d", q=2),
                            gs[:].rearrange("p (g q) h d -> p g q (h d)", q=2),
                            e.unsqueeze(3).broadcast_to([P, HG, 2, 2 * DH]), ALU.mult)
                        if r == 1:
                            ins_.then_inc(s["state_ready"], 1)

            run(dve, step, -1, 1)

        @block.gpsimd
        def _(pool):
            def stage(i, t):
                pool.tensor_copy(vt[:, t % 2], m["valueT"][:, :, bass.ds((2 * i + t) * P, P)]).then_inc(s["staged"], 1)

            def step(i, n, lo, hi):
                unit = BODY * i
                if lo <= n + 1 < hi:
                    q = n + 1
                    wait_alone(pool, s["s_copied"], 2 * (unit + q) + 2, s["pool_passed"])
                    v = pm[:, q % 2].rearrange("p a b t -> p (a b) t")
                    pool.affine_select(out=v, in_=v, compare_op=ALU.is_ge, fill=0.0, base=0, pattern=[[0, 4], [1, P]],
                                       channel_multiplier=-1).then_inc(s["masked"], 1)
                if n % HG == 2 and n + 6 < hi:
                    wait_alone(pool, s["bc_ready"], unit + n // HG * HG + 1, s["pool_passed"])
                    stage(i, n // HG + 1)

            stage(0, 0)
            run(pool, step, -1, 16)


def close(k, m, ins):
    nc = k.nc
    with ExitStack() as ctx:
        sb, sem = tools(nc, ctx)
        w = sb("w_out", P, 2, D)
        skip = sb("skip", P, DI)
        yT = sb("yT", P, 4, 2, P)
        s = {n: sem("cl_" + n) for n in ("loaded", "sk", "sum", "y", "yT_ready", "yT_taken", "o_ready", "x")}
        block = ctx.enter_context(nc.Block())

        @block.sync
        def _(sp):
            sp.dma_start(w[:], ins["w_out"].rearrange("(c p) d -> p c d", p=P)).then_inc(s["loaded"], 16)
            sp.dma_start(skip[:], ins["skip"].rearrange("(a c) -> a c", a=1).broadcast_to([P, DI])).then_inc(s["loaded"], 16)

        @block.vector
        def _(dve):
            dve.wait_ge(s["loaded"], 32)

            def residual(t):
                dve.wait_ge(s["o_ready"], t + 1)
                dve.tensor_tensor(k.x[:, t, :], k.x[:, t, :], k.bank[4 + t % 4][:, 0:D], ALU.add).then_inc(s["x"], 1)

            for t in range(TILES):
                dve.tensor_tensor(m["u"][:, t], m["u"][:, t], skip[:], ALU.mult).then_inc(s["sk"], 1)
                dve.wait_ge(s["sk"], t + 1)
                dve.tensor_tensor(m["y"][:, t], m["y"][:, t], m["u"][:, t], ALU.add).then_inc(s["sum"], 1)
                dve.wait_ge(s["sum"], t + 1)
                dve.tensor_tensor(m["y"][:, t], m["y"][:, t], m["gate"][:, t], ALU.mult).then_inc(s["y"], 1)
                if t >= 2:
                    residual(t - 2)
            residual(TILES - 2)
            residual(TILES - 1)

        @block.tensor
        def _(pe):
            def turn(t):
                pe.wait_ge(s["y"], t + 1)
                if t >= 4:
                    pe.wait_ge(s["yT_taken"], t - 3)
                for c in range(2):
                    mm = pe.transpose(k.bank[t % 4][:, c * P:(c + 1) * P], m["y"][:, t, c * P:(c + 1) * P], k.ident[:])
                mm.then_inc(s["yT_ready"], 1)

            pe.wait_ge(s["loaded"], 32)
            turn(0)
            for t in range(TILES):
                if t + 1 < TILES:
                    turn(t + 1)
                pe.wait_ge(s["yT_taken"], t + 1)
                if t >= 4:
                    pe.wait_ge(s["x"], t - 3)
                for c in range(2):
                    mm = pe.matmul(k.bank[4 + t % 4][:, 0:D], yT[:, t % 4, c], w[:, c], start=(c == 0), stop=(c == 1))
                mm.then_inc(s["o_ready"], 1)

        @block.scalar
        def _(act):
            for t in range(TILES):
                act.wait_ge(s["yT_ready"], t + 1)
                if t >= 4:
                    act.wait_ge(s["o_ready"], t - 3)
                act.copy(yT[:, t % 4].rearrange("p c t -> p (c t)"), k.bank[t % 4][:, 0:2 * P]).then_inc(s["yT_taken"], 1)


def ffn(k, ins, tag):
    nc = k.nc
    KH = HID // P
    PAIRS = B // 2
    with ExitStack() as ctx:
        sb, sem = tools(nc, ctx)
        xnT = sb(f"xnT{tag}", P, TOK)
        w12 = sb(f"w12{tag}", P, 2, HID)
        h12 = sb(f"h12{tag}", P, 2, KH, HID)
        w3 = sb(f"w3{tag}", P, KH, D)
        s12 = sb(f"s12{tag}", P, 4, KH)
        s3 = sb(f"s3{tag}", P, D)
        g = sb(f"g{tag}", P, 2, T)
        ha = sb(f"ha{tag}", P, 2, KH, T)
        hb = sb(f"hb{tag}", P, 2, KH, T)
        o = sb(f"o{tag}", P, 4, D)
        s = {n: sem(f"{n}{tag}") for n in (
            "loaded", "up_ready", "silu", "gated", "h1_ready", "gelu1", "h2_ready", "gelu2", "out_ready", "scaled", "added")}
        norm_transpose(k, xnT, "f" + tag)
        block = ctx.enter_context(nc.Block())

        @block.sync
        def _(sp):
            for j, n in enumerate(("w1", "w2")):
                sp.dma_start(w12[:, j], ins[n]).then_inc(s["loaded"], 16)
            for j, n in enumerate(("h1", "h2")):
                sp.dma_start(h12[:, j], ins[n].rearrange("(c p) o -> p c o", p=P)).then_inc(s["loaded"], 16)
            sp.dma_start(w3[:], ins["w3"].rearrange("(c p) o -> p c o", p=P)).then_inc(s["loaded"], 16)
            sp.dma_start(s12[:], ins["s12"]).then_inc(s["loaded"], 16)
            sp.dma_start(s3[:], ins["s3"].rearrange("(a d) -> a d", a=1).broadcast_to([P, D])).then_inc(s["loaded"], 16)
            sp.wait_ge(s["loaded"], 112)

        @block.tensor
        def _(pe):
            pe.sem_inc(s["out_ready"], 1)
            pe.wait_ge(s["loaded"], 112)
            with pe.Fori(0, PAIRS) as i:
                for j in range(2 * KH):
                    blk, c = divmod(j, KH)
                    if j < 4:
                        pe.wait_ge(s["gelu2"], 8 * i + 1)
                        pe.wait_ge(s["added"], 2 * i + 1)
                    else:
                        pe.wait_ge(s["gated"], 8 * i + j - 3)
                    for w in range(2):
                        mm = pe.matmul(k.bank[2 * (j % 4) + w][:], w12[:, w, c * P:(c + 1) * P],
                                       xnT[:, bass.ds((2 * i + blk) * T, T)])
                    mm.then_inc(s["up_ready"], 1)
                for layer, (src, before, ready) in enumerate(((ha, "gated", "h1_ready"), (hb, "gelu1", "h2_ready"))):
                    for j in range(2 * KH):
                        blk, c = divmod(j, KH)
                        first = max(KH * (blk + 1), j // 2 + 5) if layer == 0 else KH * (blk + 1) + 1
                        pe.wait_ge(s[before], 8 * i + first)
                        for q in range(KH):
                            mm = pe.matmul(k.bank[j][:], h12[:, layer, q, c * P:(c + 1) * P], src[:, blk, q],
                                           start=(q == 0), stop=(q == KH - 1))
                        mm.then_inc(s[ready], 1)
                for blk in range(2):
                    pe.wait_ge(s["gelu2"], 8 * i + KH * (blk + 1) + 1)
                    for t in range(TPB):
                        for q in range(KH):
                            mm = pe.matmul(k.bank[blk][:, t * D:(t + 1) * D], ha[:, blk, q, t * P:(t + 1) * P], w3[:, q],
                                           start=(q == 0), stop=(q == KH - 1))
                    mm.then_inc(s["out_ready"], 1)

        @block.scalar
        def _(act):
            act.sem_inc(s["gelu1"], 1)
            act.sem_inc(s["gelu2"], 1)
            act.wait_ge(s["loaded"], 112)
            with act.Fori(0, PAIRS) as i:
                for j in range(2 * KH):
                    act.wait_ge(s["up_ready"], 8 * i + j + 1)
                    act.wait_ge(s["gated"], 8 * i + j - 1) if j >= 2 else act.wait_ge(s["added"], 2 * i + 1)
                    act.activation(g[:, j % 2], k.bank[2 * (j % 4)][:], ACT.Silu,
                                   scale=s12[:, 0, j % KH:j % KH + 1]).then_inc(s["silu"], 1)
                for layer, (dst, ready, done) in enumerate(((hb, "h1_ready", "gelu1"), (ha, "h2_ready", "gelu2"))):
                    for j in range(2 * KH):
                        act.wait_ge(s[ready], 8 * i + j + 1)
                        if layer == 1:
                            act.wait_ge(s["h1_ready"], 8 * i + 8)
                        act.activation(dst[:, j // KH, j % KH], k.bank[j][:], ACT.Gelu,
                                       scale=s12[:, 2 + layer, j % KH:j % KH + 1]).then_inc(s[done], 1)

        @block.vector
        def _(dve):
            dve.sem_inc(s["added"], 1)
            dve.wait_ge(s["loaded"], 112)
            with dve.Fori(0, PAIRS) as i:
                for j in range(2 * KH):
                    dve.wait_ge(s["silu"], 8 * i + j + 1)
                    if j == 0:
                        dve.wait_ge(s["out_ready"], 2 * i + 1)
                    dve.scalar_tensor_tensor(out=ha[:, j // KH, j % KH], in0=k.bank[2 * (j % 4) + 1][:],
                                             scalar=s12[:, 1, j % KH:j % KH + 1], in1=g[:, j % 2], op0=ALU.mult,
                                             op1=ALU.mult).then_inc(s["gated"], 1)
                for blk in range(2):
                    dve.wait_ge(s["out_ready"], 2 * i + blk + 2)
                    dve.wait_ge(s["added"], 2 * i + blk + 1)
                    dve.tensor_tensor(o[:], k.bank[blk][:].rearrange("p (t d) -> p t d", d=D),
                                      s3[:].unsqueeze(1).broadcast_to([P, 4, D]), ALU.mult).then_inc(s["scaled"], 1)
                    dve.wait_ge(s["scaled"], 2 * i + blk + 1)
                    xv = k.x[:, bass.ds((2 * i + blk) * TPB, TPB), :]
                    dve.tensor_tensor(xv, xv, o[:], ALU.add).then_inc(s["added"], 1)


def attention(k, ins):
    nc = k.nc
    PAIRS = HEADS // 2
    UNITS = PAIRS * TPB
    with ExitStack() as ctx:
        sb, sem = tools(nc, ctx)
        xT = sb("xT", P, TOK)
        wq = sb("wq", P, INNER)
        wkv = sb("wkv", P, 2 * INNER)
        wo = sb("wo", P, PAIRS, D)
        wg = sb("wg", P, HEADS)
        sg = sb("sg", P, TILES, HEADS)
        tri = sb("tri", P, P)
        xb = sb("xb", P, T)
        v = sb("v", P, TPB, INNER)
        qT = sb("qT", P, 2, T)
        kT = sb("kT", P, 2, T)
        mx = sb("mx", P, 2, 2)
        nm = sb("nm", P, 2, 2)
        sm = sb("sm", P, 4, 2)
        fac = sb("fac", P, 2)
        pr = sb("pr", P, 2, 2, T)
        prT = sb("prT", P, 2, 2, T)
        att = sb("att", P, TPB, INNER)
        attT = sb("attT", P, 2, PAIRS, P)
        s = {n: sem("at_" + n) for n in (
            "loaded", "tri0", "tri", "g_ready", "gate", "staged", "v_ready", "v_copied", "p_ready", "p_copied",
            "s_ready", "masked", "max", "neg", "exped", "tr_ready", "tr_copied", "pv_ready", "rec", "fac", "o_scaled",
            "t_ready", "t_copied", "o_ready", "added", "pool_passed")}
        norm_transpose(k, xT, "a", rms_weight=ins["norm_w"])
        S = [[k.bank[0], k.bank[1]], [k.bank[2], k.bank[3]]]
        TR, OB, PJ = [k.bank[4], k.bank[5]], k.bank[6], k.bank[7]
        VB = [k.bank[n] for n in range(4)]
        block = ctx.enter_context(nc.Block())

        @block.sync
        def _(sp):
            sp.dma_start(wq[:], ins["wq"]).then_inc(s["loaded"], 16)
            sp.dma_start(wkv[:], ins["wkv"]).then_inc(s["loaded"], 16)
            sp.dma_start(wo[:], ins["wo"].rearrange("(c p) d -> p c d", p=P)).then_inc(s["loaded"], 16)
            sp.dma_start(wg[:], ins["wg"]).then_inc(s["loaded"], 16)
            sp.wait_ge(s["loaded"], 64)

        @block.gpsimd
        def _(pool):
            pool.memset(tri[:], 0.0).then_inc(s["tri0"], 1)
            pool.wait_ge(s["tri0"], 1)
            pool.affine_select(out=tri[:], in_=tri[:], compare_op=ALU.is_ge, fill=MASKED, base=0, pattern=[[-1, P]],
                               channel_multiplier=1).then_inc(s["tri"], 1)
            with pool.Fori(0, B) as b:
                wait_alone(pool, s["p_ready"], 2 * PAIRS * b + 1, s["pool_passed"])
                pool.tensor_copy(xb[:], xT[:, bass.ds(T * b, T)]).then_inc(s["staged"], 1)

        @block.tensor
        def _(pe):
            pe.sem_inc(s["p_ready"], 1)
            pe.sem_inc(s["pv_ready"], 2)
            pe.wait_ge(s["loaded"], 64)
            for t in range(TILES):
                mm = pe.matmul(k.bank[7][:, t * HEADS:(t + 1) * HEADS], xT[:, t * P:(t + 1) * P], wg[:])
            mm.then_inc(s["g_ready"], 1)
            with pe.Fori(0, B) as b:
                base = UNITS * b

                def projection(pair, which):
                    n = 2 * pair + which
                    pe.wait_ge(s["p_copied"], 2 * PAIRS * b + n + 1)
                    w = (wq, wkv)[which]
                    pe.matmul(PJ[:], w[:, pair * P:(pair + 1) * P], xb[:]).then_inc(s["p_ready"], 1)

                pe.wait_ge(s["staged"], b + 1)
                for j in range(2 * TPB):
                    t, half = divmod(j, 2)
                    if j < 4:
                        pe.wait_ge(s["t_copied"], 2 * TPB * b + 1)
                    else:
                        pe.wait_ge(s["v_copied"], 2 * TPB * b + j - 3)
                    pe.matmul(VB[j % 4][:], xb[:, t * P:(t + 1) * P],
                              wkv[:, INNER + half * 512:INNER + (half + 1) * 512]).then_inc(s["v_ready"], 1)
                projection(0, 0)
                projection(0, 1)
                for n in range(UNITS + 2):
                    if n < UNITS:
                        pair, it = divmod(n, TPB)
                        w = (it + 1) * P
                        if it == 0:
                            pe.wait_ge(s["p_copied"], 2 * PAIRS * b + 2 * pair + 3)
                        if n < 2:
                            pe.wait_ge(s["v_copied"], 2 * TPB * b + 2 * TPB)
                        pe.wait_ge(s["exped"], 2 * (base + n) + 2)
                        for h in range(2):
                            lane = slice(64 * h, 64 * h + 64)
                            mm = pe.matmul(S[n % 2][h][:, 0:w], qT[lane, pair % 2, it * P:(it + 1) * P],
                                           kT[lane, pair % 2, 0:w])
                        mm.then_inc(s["s_ready"], 1)
                        if it in (1, 2) and pair + 1 < PAIRS:
                            projection(pair + 1, it - 1)
                    if 1 <= n <= UNITS:
                        q = n - 1
                        it = q % TPB
                        pe.wait_ge(s["exped"], 2 * (base + q) + 6)
                        pe.wait_ge(s["tr_copied"], 2 * (base + q) + 1)
                        for h in range(2):
                            for j in range(it + 1):
                                mm = pe.transpose(TR[h][:, j * P:(j + 1) * P], pr[:, q % 2, h, j * P:(j + 1) * P],
                                                  k.ident[:])
                        mm.then_inc(s["tr_ready"], 1)
                    if n >= 2:
                        q = n - 2
                        pair, it = divmod(q, TPB)
                        pe.wait_ge(s["tr_copied"], 2 * (base + q) + 3)
                        pe.wait_ge(s["o_scaled"], base + q + 1)
                        for h in range(2):
                            for j in range(it + 1):
                                c0 = (2 * pair + h) * DHEAD
                                mm = pe.matmul(OB[:, h * DHEAD:(h + 1) * DHEAD], prT[:, q % 2, h, j * P:(j + 1) * P],
                                               v[:, j, c0:c0 + DHEAD], start=(j == 0), stop=(j == it))
                        mm.then_inc(s["pv_ready"], 1)
                for t in range(TPB + 1):
                    if t < TPB:
                        if t == 0:
                            pe.wait_ge(s["o_scaled"], base + UNITS + 1)
                        if t >= 2:
                            pe.wait_ge(s["t_copied"], 2 * (TPB * b + t) - 1)
                        for c in range(PAIRS):
                            mm = pe.transpose(S[t % 2][c // 4][:, c % 4 * P:(c % 4 + 1) * P], att[:, t, c * P:(c + 1) * P],
                                              k.ident[:])
                        mm.then_inc(s["t_ready"], 1)
                    if t >= 1:
                        q = t - 1
                        pe.wait_ge(s["t_copied"], 2 * (TPB * b + q) + 3)
                        if q >= 2:
                            pe.wait_ge(s["added"], TPB * b + q - 1)
                        for c in range(PAIRS):
                            mm = pe.matmul(TR[q % 2][:, 0:D], attT[:, q % 2, c], wo[:, c], start=(c == 0),
                                           stop=(c == PAIRS - 1))
                        mm.then_inc(s["o_ready"], 1)

        @block.scalar
        def _(act):
            act.sem_inc(s["exped"], 4)
            act.sem_inc(s["tr_copied"], 1)
            act.sem_inc(s["p_copied"], 1)
            act.sem_inc(s["t_copied"], 1)
            act.wait_ge(s["g_ready"], 1)
            act.activation(sg[:].rearrange("p t h -> p (t h)"), k.bank[7][:, 0:TILES * HEADS], ACT.Sigmoid
                           ).then_inc(s["gate"], 1)
            act.wait_ge(s["gate"], 1)
            with act.Fori(0, B) as b:
                base = UNITS * b

                def projected(pair, which):
                    act.wait_ge(s["p_ready"], 2 * PAIRS * b + 2 * pair + which + 2)
                    if which == 0:
                        act.mul(qT[:, pair % 2], PJ[:], DHEAD ** -0.5).then_inc(s["p_copied"], 1)
                    else:
                        act.copy(kT[:, pair % 2], PJ[:]).then_inc(s["p_copied"], 1)

                for j in range(2 * TPB):
                    act.wait_ge(s["v_ready"], 2 * TPB * b + j + 1)
                    act.copy(v[:, j // 2, j % 2 * 512:(j % 2 + 1) * 512], VB[j % 4][:]).then_inc(s["v_copied"], 1)
                projected(0, 0)
                projected(0, 1)
                for n in range(UNITS + 1):
                    if n < UNITS:
                        pair, it = divmod(n, TPB)
                        w = (it + 1) * P
                        act.wait_ge(s["neg"], base + n + 1)
                        act.wait_ge(s["tr_ready"], base + n) if n >= 2 else act.wait_ge(s["v_ready"], 2 * TPB * b + 1)
                        act.wait_ge(s["pv_ready"], base + n) if n >= 1 else act.wait_ge(s["pv_ready"], base + 1)
                        for h in range(2):
                            act.activation(pr[:, n % 2, h, 0:w], S[n % 2][h][:, 0:w], ACT.Exp, bias=nm[:, n % 2, h:h + 1],
                                           accum_out=sm[:, n % 4, h:h + 1]).then_inc(s["exped"], 1)
                        if it in (1, 2) and pair + 1 < PAIRS:
                            projected(pair + 1, it - 1)
                    if n >= 1:
                        q = n - 1
                        w = (q % TPB + 1) * P
                        act.wait_ge(s["tr_ready"], base + q + 1)
                        act.wait_ge(s["pv_ready"], base + q + 1)
                        for h in range(2):
                            act.copy(prT[:, q % 2, h, 0:w], TR[h][:, 0:w]).then_inc(s["tr_copied"], 1)
                for t in range(TPB):
                    act.wait_ge(s["t_ready"], TPB * b + t + 1)
                    if t >= 2:
                        act.wait_ge(s["o_ready"], TPB * b + t - 1)
                    for c in range(2):
                        act.copy(attT[:, t % 2, 4 * c:4 * c + 4].rearrange("p c i -> p (c i)"), S[t % 2][c][:]
                                 ).then_inc(s["t_copied"], 1)

        @block.vector
        def _(dve):
            dve.sem_inc(s["o_scaled"], 1)
            dve.wait_ge(s["tri"], 1)
            dve.wait_ge(s["gate"], 1)
            with dve.Fori(0, B) as b:
                base = UNITS * b
                for n in range(UNITS + 2):
                    if n < UNITS:
                        pair, it = divmod(n, TPB)
                        w = (it + 1) * P
                        dve.wait_ge(s["s_ready"], base + n + 1)
                        for h in range(2):
                            diag = S[n % 2][h][:, it * P:w]
                            dve.tensor_tensor(diag, diag, tri[:], ALU.add).then_inc(s["masked"], 1)
                        for h in range(2):
                            dve.wait_ge(s["masked"], 2 * (base + n) + 1 + h)
                            dve.tensor_reduce(mx[:, n % 2, h:h + 1], S[n % 2][h][:, 0:w], AX.X, ALU.max).then_inc(s["max"], 1)
                        dve.wait_ge(s["max"], 2 * (base + n) + 2)
                        dve.wait_ge(s["exped"], 2 * (base + n) + 2)
                        dve.tensor_scalar(nm[:, n % 2], mx[:, n % 2], -1.0, None, ALU.mult).then_inc(s["neg"], 1)
                    if n >= 2:
                        q = n - 2
                        pair, it = divmod(q, TPB)
                        dve.wait_ge(s["exped"], 2 * (base + q) + 6)
                        dve.reciprocal(fac[:], sm[:, q % 4]).then_inc(s["rec"], 1)
                        dve.wait_ge(s["rec"], base + q + 1)
                        dve.tensor_tensor(fac[:], fac[:], sg[:, TPB * b + it, 2 * pair:2 * pair + 2], ALU.mult
                                          ).then_inc(s["fac"], 1)
                        dve.wait_ge(s["fac"], base + q + 1)
                        dve.wait_ge(s["pv_ready"], base + q + 3)
                        dve.tensor_tensor(att[:, it, pair * P:(pair + 1) * P].rearrange("p (h d) -> p h d", h=2),
                                          OB[:, 0:P].rearrange("p (h d) -> p h d", h=2),
                                          fac[:].unsqueeze(2).broadcast_to([P, 2, DHEAD]), ALU.mult).then_inc(s["o_scaled"], 1)
                        dve.wait_ge(s["o_scaled"], base + q + 2)
                for t in range(TPB):
                    dve.wait_ge(s["o_ready"], TPB * b + t + 1)
                    xv = k.x[:, bass.ds(TPB * b + t, 1), :].rearrange("p a d -> p (a d)")
                    dve.tensor_tensor(xv, xv, TR[t % 2][:, 0:D], ALU.add).then_inc(s["added"], 1)


def store(k, out):
    nc = k.nc
    with ExitStack() as ctx:
        sb, sem = tools(nc, ctx)
        out_stored = sem("out_stored")
        block = ctx.enter_context(nc.Block())

        @block.sync
        def _(sp):
            sp.dma_start(out.rearrange("(t p) d -> p t d", p=P), k.x[:]).then_inc(out_stored, 16)
            sp.wait_ge(out_stored, 16)


def build(nc, a, out, debug):
    with ExitStack() as ctx:
        k = Kernel(nc, ctx, debug)
        psi = nc.dram_tensor("psi", [P, P + 1, REC], F32, kind="ExternalOutput" if debug else "Internal").ap()
        par = nc.dram_tensor("par_scratch", [2 * H, TOK], F32, kind="Internal").ap()
        scratch = {"psi": psi, "par": par}
        load_and_identity(k, a["x"])
        with ExitStack() as mctx:
            sb, sem = tools(nc, mctx)
            m = {"valueT": sb("valueT", P, 2, TOK), "u": sb("u", P, TILES, DI), "gate": sb("gate", P, TILES, DI),
                 "dt": sb("dt", P, TILES, H), "enter": sb("enter", P, 4, HG, TILES)}
            project(k, m, a, scratch)
            recur(k, m, a, scratch)
            m["y"] = sb("y", P, TILES, DI)
            mix(k, m, a, scratch)
            close(k, m, a)
            if debug:
                dump(k, m, out)
        ffn(k, {n: a["f0_" + n] for n in FFN_INS}, "A")
        attention(k, a)
        ffn(k, {n: a["f1_" + n] for n in FFN_INS}, "B")
        store(k, out)


def dump(k, m, out):
    nc = k.nc
    with ExitStack() as ctx:
        sb, sem = tools(nc, ctx)
        d = sem("dumped")
        block = ctx.enter_context(nc.Block())

        @block.sync
        def _(sp):
            n = 0
            for name, t in m.items():
                if name == "valueT": continue
                o = k.nc.dram_tensor("dbg_" + name, list(t.shape), F32, kind="ExternalOutput").ap()
                sp.dma_start(o, t[:]).then_inc(d, 16)
                n += 16
            o = nc.dram_tensor("x1", [P, TILES, D], F32, kind="ExternalOutput").ap()
            sp.dma_start(o, k.x[:]).then_inc(d, 16)
            sp.wait_ge(d, n + 16)


FFN_INS = ("w1", "w2", "h1", "h2", "w3", "s12", "s3")


DEBUG = False


def kernel(**inputs):
    import numpy as np
    import concourse.bacc as bacc
    from concourse.bass_utils import run_bass_kernel_spmd as run

    i = {n: np.ascontiguousarray(v) for n, v in inputs.items()}
    wi = i["L0_attn_W_in"]
    par = wi[2 * DI:].reshape(H, 2, D)
    w_in = np.concatenate([wi[:DI], par[:, 0], par[:, 1], wi[DI:2 * DI]], axis=0)
    arrays = {
        "x": i["L0_attn_x"].reshape(TOK, D),
        "w_in": np.ascontiguousarray(w_in.T),
        "dw": i["L0_attn_dw_weight"],
        "db": np.ascontiguousarray(i["L0_attn_dw_bias"].reshape(2, P).T),
        "w_bc": np.ascontiguousarray(i["L0_attn_W_bc"].T),
        "w_out": np.ascontiguousarray(i["L0_attn_W_out"].T),
        "skip": i["L0_attn_skip"],
        "A_log": i["L0_attn_A_log"],
        "dt_bias": i["L0_attn_dt_bias"],
        "norm_w": i["L1_attn_norm_w"].reshape(D, 1),
        "wq": i["L1_attn_Wq"],
        "wkv": i["L1_attn_Wkv"],
        "wo": i["L1_attn_Wout"],
        "wg": i["L1_attn_Wg"],
    }
    for layer in range(2):
        f = {n: i[f"L{layer}_ffn_{n}"] for n in (w + e for w in ("w1", "w2", "h1", "h2", "w3") for e in ("_w", "_s"))}
        for w in ("w1", "w2", "h1", "h2", "w3"):
            arrays[f"f{layer}_{w}"] = np.ascontiguousarray(f[w + "_w"].T)
        s12 = np.stack([f[w + "_s"].reshape(HID // P, P) for w in ("w1", "w2", "h1", "h2")])
        arrays[f"f{layer}_s12"] = np.ascontiguousarray(s12.transpose(2, 0, 1))
        arrays[f"f{layer}_s3"] = f["w3_s"]
    nc = bacc.Bacc("TRN2", target_bir_lowering=False, num_devices=1)
    aps = {n: nc.dram_tensor("in_" + n, v.shape, F32, kind="ExternalInput").ap() for n, v in arrays.items()}
    out = nc.dram_tensor("out_0", [TOK, D], F32, kind="ExternalOutput").ap()
    build(nc, aps, out, DEBUG)
    r = run(nc, [{"in_" + n: v for n, v in arrays.items()}], core_ids=[0])
    return r.results[0]["out_0"].reshape(B, T, D)
```

```python
from contextlib import ExitStack

import concourse.bass as bass
from concourse import mybir

F32 = mybir.dt.float32
ACT = mybir.ActivationFunctionType
ALU = mybir.AluOpType
AX = mybir.AxisListType

P = 128
B, T, D = 4, 512, 128
TOK = B * T
TILES = TOK // P
TPB = T // P
DI, H, N, KC = 256, 32, 32, 4
DH = DI // H
G4 = 4
HG = H // G4
HN = G4 * N
REC = 5 * HN
STEPS = 16
HID = 512
HEADS, DHEAD = 16, 64
INNER = HEADS * DHEAD
DT_MIN, DT_MAX, K_MAX, NORM_EPS, LN_EPS = 1e-4, 0.1, 0.5, 1e-8, 1e-5
RMS_EPS = 1.1920928955078125e-07
MASKED = -1e30


class Kernel:

    def __init__(self, nc, ctx, debug):
        self.nc = nc
        self.debug = debug
        self.bank = [ctx.enter_context(nc.psum_tensor(f"bank{i}", [P, 512], F32)) for i in range(8)]
        self.x = ctx.enter_context(nc.sbuf_tensor("x", [P, TILES, D], F32))
        self.ident = ctx.enter_context(nc.sbuf_tensor("ident", [P, P], F32))


def tools(nc, ctx):
    sems = []

    def clear():
        if sems:
            nc.clear_and_free_semaphores(sems)
            nc.all_engine_barrier()

    ctx.callback(clear)

    def sb(name, *shape):
        return ctx.enter_context(nc.sbuf_tensor(name, list(shape), F32))

    def sem(name):
        sems.append(nc.alloc_semaphore(name))
        return sems[-1]

    return sb, sem


def load_and_identity(k, x_in):
    nc = k.nc
    with ExitStack() as ctx:
        sb, sem = tools(nc, ctx)
        x_loaded, cleared, ident_made = sem("x_loaded"), sem("id_cleared"), sem("ident_made")
        block = ctx.enter_context(nc.Block())

        @block.sync
        def _(sp):
            sp.dma_start(k.x[:], x_in.rearrange("(t p) d -> p t d", p=P)).then_inc(x_loaded, 16)
            sp.wait_ge(x_loaded, 16)

        @block.gpsimd
        def _(pool):
            pool.memset(k.ident[:], 0.0).then_inc(cleared, 1)
            pool.wait_ge(cleared, 1)
            pool.affine_select(out=k.ident[:], in_=k.ident[:], compare_op=ALU.not_equal, fill=1.0, base=0,
                               pattern=[[-1, P]], channel_multiplier=1).then_inc(ident_made, 1)


def wait_alone(eng, sem, value, passed):
    eng.wait_ge(sem, value)
    eng.sem_inc(passed)


def norm_transpose(k, xnT, tag, rms_weight=None):
    nc = k.nc
    with ExitStack() as ctx:
        sb, sem = tools(nc, ctx)
        stats = sb(f"stats{tag}", P, TILES, 6)
        mv = sb(f"mv{tag}", P, TILES, 2)
        std = sb(f"std{tag}", P, TILES)
        rstd = sb(f"rstd{tag}", P, TILES)
        xn = sb(f"xn{tag}", P, TILES, D)
        stats_made, mv_made, var_eps, std_made = (sem(f"{s}{tag}") for s in ("stats", "mv", "vare", "std"))
        rstd_made, xn_made, xnT_ready, xnT_taken = (sem(f"{s}{tag}") for s in ("rstd", "xn", "xnTr", "xnTt"))
        if rms_weight is not None:
            nw = sb(f"nw{tag}", P, 1)
            sq = sb(f"sq{tag}", P, 2, D)
            ms = sb(f"ms{tag}", P, TILES)
            rms = sb(f"rms{tag}", P, TILES)
            nw_loaded, sq_made, ms_eps, rms_std, rms_made, xr_made = (
                sem(f"{s}{tag}") for s in ("nwl", "sqm", "mse", "rmss", "rmsm", "xrm"))
        block = ctx.enter_context(nc.Block())

        @block.sync
        def _(sp):
            if rms_weight is not None:
                sp.dma_start(nw[:], rms_weight).then_inc(nw_loaded, 16)
                sp.wait_ge(nw_loaded, 16)

        @block.vector
        def _(dve):
            with dve.Fori(0, TILES) as t:
                dve.bn_stats(stats[:, t, :], k.x[:, t, :]).then_inc(stats_made, 1)
            dve.wait_ge(stats_made, TILES)
            for t in range(TILES):
                dve.bn_aggr(mv[:, t, :], stats[:, t, :]).then_inc(mv_made, 1)
            dve.wait_ge(mv_made, TILES)
            dve.tensor_scalar(std[:], mv[:, :, 1], LN_EPS, None, ALU.add).then_inc(var_eps, 1)
            dve.wait_ge(std_made, 1)
            dve.reciprocal(rstd[:], std[:]).then_inc(rstd_made, 1)
            dve.wait_ge(rstd_made, 1)
            for t in range(TILES):
                dve.tensor_scalar(xn[:, t, :], k.x[:, t, :], mv[:, t, 0:1], rstd[:, t:t + 1],
                                  ALU.subtract, ALU.mult).then_inc(xn_made, 1)
            if rms_weight is not None:
                dve.wait_ge(sq_made, TILES)
                dve.tensor_scalar(rms[:], ms[:], 1.0 / D, RMS_EPS, ALU.mult, ALU.add).then_inc(ms_eps, 1)
                dve.wait_ge(rms_std, 1)
                dve.reciprocal(rms[:], ms[:]).then_inc(rms_made, 1)
                dve.wait_ge(rms_made, 1)
                for t in range(TILES):
                    dve.tensor_scalar(xn[:, t, :], xn[:, t, :], rms[:, t:t + 1], None,
                                      ALU.mult).then_inc(xr_made, 1)

        @block.tensor
        def _(pe):
            for t in range(TILES):
                pe.wait_ge(xn_made if rms_weight is None else xr_made, t + 1)
                if t % 4 == 0 and t >= 8:
                    pe.wait_ge(xnT_taken, t // 4 - 1)
                pe.transpose(k.bank[t // 4 % 2][:, t % 4 * P:(t % 4 + 1) * P], xn[:, t, :],
                             k.ident[:]).then_inc(xnT_ready, 1)

        @block.scalar
        def _(act):
            act.wait_ge(var_eps, 1)
            act.activation(std[:], std[:], ACT.Sqrt).then_inc(std_made, 1)
            if rms_weight is not None:
                for t in range(TILES):
                    act.wait_ge(xn_made, t + 1)
                    if t >= 2:
                        act.wait_ge(sq_made, t - 1)
                    act.activation(sq[:, t % 2, :], xn[:, t, :], ACT.Square,
                                   accum_out=ms[:, t:t + 1]).then_inc(sq_made, 1)
                act.wait_ge(ms_eps, 1)
                act.activation(ms[:], rms[:], ACT.Sqrt).then_inc(rms_std, 1)
                act.wait_ge(nw_loaded, 16)
            for g in range(TILES // 4):
                act.wait_ge(xnT_ready, 4 * g + 4)
                scale = 1.0 if rms_weight is None else nw[:, 0:1]
                act.activation(xnT[:, g * 512:(g + 1) * 512], k.bank[g % 2][:], ACT.Copy,
                               scale=scale).then_inc(xnT_taken, 1)


def project(k, m, ins, scratch):
    nc = k.nc
    with ExitStack() as ctx:
        sb, sem = tools(nc, ctx)
        NW = DI + 2 * H
        w_in = sb("w_in", P, NW + DI)
        xnT = sb("xnT", P, TOK)
        raw = sb("raw_value", P, 2, B, T + KC - 1)
        conv = sb("conv", P, 2, TOK)
        par = sb("par", 2 * H, TOK)
        dw = sb("dw", P, 2, KC)
        db = sb("db", P, 2)
        dtb = sb("dtb", P, H)
        soft = sb("soft", P, 3, TILES * H)
        norm_transpose(k, xnT, "0")
        s = {n: sem("pj_" + n) for n in (
            "loaded", "ready", "taken", "padded", "conv", "value", "uT_ready", "uT_taken", "par_stored",
            "dt_biased", "abs", "exp", "ln", "relu", "sum", "clip")}
        block = ctx.enter_context(nc.Block())
        NJ = B + 2 * B + TILES

        @block.sync
        def _(sp):
            sp.dma_start(w_in[:], ins["w_in"]).then_inc(s["loaded"], 16)
            sp.dma_start(dw[:], ins["dw"].rearrange("(c p) k -> p c k", p=P)).then_inc(s["loaded"], 16)
            sp.dma_start(db[:], ins["db"]).then_inc(s["loaded"], 16)
            sp.dma_start(dtb[:], ins["dt_bias"].rearrange("(a h) -> a h", a=1).broadcast_to([P, H])).then_inc(s["loaded"], 16)
            sp.wait_ge(s["taken"], B)
            sp.dma_start(scratch["par"], par[:]).then_inc(s["par_stored"], 16)
            sp.wait_ge(s["par_stored"], 16)

        @block.tensor
        def _(pe):
            pe.wait_ge(s["loaded"], 64)
            for j in range(NJ):
                if j >= 4:
                    pe.wait_ge(s["taken"], j - 3)
                out = k.bank[j % 4]
                if j < B:
                    ins_ = pe.matmul(out[0:2 * H, :], w_in[:, DI:NW], xnT[:, j * T:(j + 1) * T])
                elif j < 3 * B:
                    c, b = divmod(j - B, B)
                    ins_ = pe.matmul(out[:], w_in[:, NW + c * P:NW + (c + 1) * P], xnT[:, b * T:(b + 1) * T])
                else:
                    t = j - 3 * B
                    ins_ = pe.matmul(out[:, 0:DI + H], xnT[:, t * P:(t + 1) * P], w_in[:, 0:DI + H])
                ins_.then_inc(s["ready"], 1)
            for g in range(TILES // 2):
                if g >= 4:
                    pe.wait_ge(s["uT_taken"], g - 3)
                for q in range(4):
                    t, c = 2 * g + q // 2, q % 2
                    pe.wait_ge(s["value"], (t // TPB) * 2 + c + 1)
                    ins_ = pe.transpose(k.bank[4 + g % 4][:, q * P:(q + 1) * P], m["valueT"][:, c, t * P:(t + 1) * P],
                                        k.ident[:])
                ins_.then_inc(s["uT_ready"], 1)

        @block.scalar
        def _(act):
            for j in range(NJ):
                act.wait_ge(s["ready"], j + 1)
                src = k.bank[j % 4]
                if j < B:
                    act.copy(par[:, j * T:(j + 1) * T], src[0:2 * H, :]).then_inc(s["taken"], 1)
                elif j < 3 * B:
                    c, b = divmod(j - B, B)
                    act.copy(raw[:, c, b, KC - 1:], src[:]).then_inc(s["taken"], 1)
                else:
                    t = j - 3 * B
                    act.copy(m["dt"][:, t, :], src[:, DI:DI + H])
                    act.activation(m["gate"][:, t, :], src[:, 0:DI], ACT.Silu).then_inc(s["taken"], 1)
            for n in range(2 * B):
                b, c = divmod(n, 2)
                act.wait_ge(s["conv"], KC * (n + 1))
                act.activation(m["valueT"][:, c, b * T:(b + 1) * T], conv[:, c, b * T:(b + 1) * T],
                               ACT.Silu).then_inc(s["value"], 1)
            for g in range(TILES // 2):
                act.wait_ge(s["uT_ready"], g + 1)
                act.copy(m["u"][:, 2 * g:2 * g + 2, :].rearrange("p t c -> p (t c)"),
                         k.bank[4 + g % 4][:]).then_inc(s["uT_taken"], 1)
            act.wait_ge(s["dt_biased"], 1)
            act.activation(soft[:, 1, :], soft[:, 0, :], ACT.Abs).then_inc(s["abs"], 1)
            act.wait_ge(s["abs"], 1)
            act.activation(soft[:, 1, :], soft[:, 1, :], ACT.Exp, scale=-1.0).then_inc(s["exp"], 1)
            act.wait_ge(s["exp"], 1)
            act.activation(soft[:, 2, :], soft[:, 1, :], ACT.Ln, bias=1.0).then_inc(s["ln"], 1)

        @block.vector
        def _(dve):
            dve.memset(raw[:, :, :, 0:KC - 1], 0.0).then_inc(s["padded"], 1)
            dve.wait_ge(s["padded"], 1)
            dve.wait_ge(s["loaded"], 64)
            for n in range(2 * B):
                b, c = divmod(n, 2)
                dve.wait_ge(s["taken"], B + c * B + b + 1)
                acc = conv[:, c, b * T:(b + 1) * T]
                dve.tensor_scalar(acc, raw[:, c, b, 0:T], dw[:, c, 0:1], db[:, c:c + 1], ALU.mult,
                                  ALU.add).then_inc(s["conv"], 1)
                for tap in range(1, KC):
                    dve.wait_ge(s["conv"], KC * n + tap)
                    dve.scalar_tensor_tensor(out=acc, in0=raw[:, c, b, tap:tap + T], scalar=dw[:, c, tap:tap + 1],
                                             in1=acc, op0=ALU.mult, op1=ALU.add).then_inc(s["conv"], 1)
            dve.wait_ge(s["taken"], NJ)
            v = soft[:, 0, :].rearrange("p (t h) -> p t h", h=H)
            dve.tensor_tensor(v, m["dt"][:], dtb[:].unsqueeze(1).broadcast_to([P, TILES, H]),
                              ALU.add).then_inc(s["dt_biased"], 1)
            dve.wait_ge(s["ln"], 1)
            dve.tensor_scalar(soft[:, 1, :], soft[:, 0, :], 0.0, None, ALU.max).then_inc(s["relu"], 1)
            dve.wait_ge(s["relu"], 1)
            dve.tensor_tensor(soft[:, 1, :], soft[:, 1, :], soft[:, 2, :], ALU.add).then_inc(s["sum"], 1)
            dve.wait_ge(s["sum"], 1)
            dve.tensor_scalar(m["dt"][:].rearrange("p t h -> p (t h)"), soft[:, 1, :], DT_MIN, DT_MAX, ALU.max,
                              ALU.min).then_inc(s["clip"], 1)


def recur(k, m, ins, scratch):
    nc = k.nc
    with ExitStack() as ctx:
        sb, sem = tools(nc, ctx)
        SLOTS = 2 * STEPS
        X = sb("X", P, SLOTS, REC)
        praw = sb("praw", P, 2, G4, P)
        coef = sb("coef", P, 4, G4, P)
        tmp = sb("ctmp", P, 3, G4 * P)
        A = sb("A", P, HN)
        dtb = sb("dtb2", P, G4)
        a = sb("a", P, 2, STEPS, HN)
        g = sb("g", P, 2, STEPS + 1, HN)
        d0 = sb("d0", P, STEPS, HN)
        t1 = sb("t1", P, 2 * HN)
        t23 = sb("t23", P, 4 * HN)
        phi = sb("phi_rows", P, 2, 2, P)
        s = {n: sem("rc_" + n) for n in (
            "pool_passed", "sp_passed", "loaded", "prep", "aexp", "start", "id_stored", "a_ready", "a_used", "rec", "g1", "g_ready", "gch", "ln",
            "d0", "n1", "n2", "det", "phi", "phiT", "phi_copied", "phi_done", "sigm")}
        stored = [sem(f"rc_stored{h}") for h in range(2)]
        block = ctx.enter_context(nc.Block())
        coef_r = coef[:].rearrange("p c h t -> p (c h) t")

        @block.sync
        def _(sp):
            n = 0
            for hg in range(HG):
                lanes = slice(hg * TILES, (hg + 1) * TILES)
                for kind in range(2):
                    src = scratch["par"][kind * H + hg * G4:kind * H + (hg + 1) * G4, :]
                    sp.dma_start(praw[lanes, kind], src.rearrange("h (c t) -> c h t", t=P)).then_inc(s["loaded"], 16)
                al = ins["A_log"][hg * G4:(hg + 1) * G4, :].rearrange("h n -> (h n)").unsqueeze(0)
                sp.dma_start(A[lanes, :], al.broadcast_to([TILES, HN])).then_inc(s["loaded"], 16)
                bl = ins["dt_bias"][hg * G4:(hg + 1) * G4].unsqueeze(0)
                sp.dma_start(dtb[lanes, :], bl.broadcast_to([TILES, G4])).then_inc(s["loaded"], 16)
                n += 4
            for h in range(2):
                sp.sem_inc(stored[h], 16)
            sp.wait_ge(s["start"], 2)
            sp.dma_start(scratch["psi"][:, 0, 0:4 * HN], X[:, SLOTS - 1, 0:4 * HN]).then_inc(s["id_stored"], 16)
            with sp.Fori(0, P // SLOTS) as i:
                for h in range(2):
                    wait_alone(sp, s["rec"], SLOTS * 4 * i + (h + 1) * STEPS * 4 + 1, s["sp_passed"])
                    wait_alone(sp, s["det"], 2 * i + h + 2, s["sp_passed"])
                    sp.dma_start(scratch["psi"][:, bass.ds(1 + SLOTS * i + h * STEPS, STEPS), :],
                                 X[:, h * STEPS:(h + 1) * STEPS, :]).then_inc(stored[h], 16)
            for h in range(2):
                sp.wait_ge(stored[h], 16 * (P // SLOTS) + 16)
            sp.wait_ge(s["id_stored"], 16)

        LOADED = 16 * 4 * HG

        @block.scalar
        def _(act):
            act.wait_ge(s["loaded"], LOADED)
            act.activation(A[:], A[:], ACT.Exp).then_inc(s["aexp"], 1)
            act.wait_ge(s["prep"], 1)
            act.activation(tmp[:, 1, :], tmp[:, 0, :], ACT.Abs).then_inc(s["sigm"], 1)
            act.wait_ge(s["sigm"], 1)
            act.activation(tmp[:, 1, :], tmp[:, 1, :], ACT.Exp, scale=-1.0).then_inc(s["sigm"], 1)
            act.wait_ge(s["sigm"], 2)
            act.activation(tmp[:, 1, :], tmp[:, 1, :], ACT.Ln, bias=1.0).then_inc(s["sigm"], 1)
            act.activation(tmp[:, 2, :], praw[:, 1].rearrange("p h t -> p (h t)"), ACT.Exp,
                           scale=-1.0).then_inc(s["sigm"], 1)
            with act.Fori(0, P // SLOTS) as i:
                for h in range(2):
                    act.wait_ge(s["g_ready"], (2 * i + h + 1) * STEPS)
                    act.wait_ge(s["det"], 2 * i + h + 1)
                    act.activation(d0[:], g[:, h, 1:], ACT.Ln).then_inc(s["ln"], 1)
                    act.wait_ge(s["ln"], 2 * i + h + 1)
                    act.activation(d0[:], d0[:], ACT.Exp, scale=-1.0).then_inc(s["d0"], 1)

        @block.vector
        def _(dve):
            rec = s["rec"]
            dve.sem_inc(rec, 1)
            dve.memset(X[:, SLOTS - 1, 0:4 * HN], 0.0).then_inc(s["start"], 1)
            dve.wait_ge(s["start"], 1)
            ends = X[:, SLOTS - 1, 0:4 * HN].rearrange("p (c n) -> p c n", n=HN)[:, 0:4:3, :]
            dve.memset(ends, 1.0).then_inc(s["start"], 1)
            dve.wait_ge(s["loaded"], LOADED)
            v = tmp[:, 0, :].rearrange("p (h t) -> p h t", t=P)
            dve.tensor_tensor(v, praw[:, 0], dtb[:].unsqueeze(2).broadcast_to([P, G4, P]), ALU.add).then_inc(s["prep"], 1)
            dve.wait_ge(s["sigm"], 4)
            dve.wait_ge(s["prep"], 1)
            dve.tensor_scalar(tmp[:, 0, :], tmp[:, 0, :], 0.0, None, ALU.max).then_inc(s["prep"], 1)
            dve.wait_ge(s["prep"], 2)
            dve.tensor_tensor(tmp[:, 0, :], tmp[:, 0, :], tmp[:, 1, :], ALU.add).then_inc(s["prep"], 1)
            dve.wait_ge(s["prep"], 3)
            dve.tensor_scalar(coef[:, 0].rearrange("p h t -> p (h t)"), tmp[:, 0, :], DT_MIN, DT_MAX, ALU.max,
                              ALU.min).then_inc(s["prep"], 1)
            dve.tensor_scalar(tmp[:, 2, :], tmp[:, 2, :], 1.0, None, ALU.add).then_inc(s["prep"], 1)
            dve.wait_ge(s["prep"], 5)
            dve.reciprocal(tmp[:, 1, :], tmp[:, 2, :]).then_inc(s["prep"], 1)
            dve.tensor_copy(coef[:, 1], coef[:, 0]).then_inc(s["prep"], 1)
            dve.wait_ge(s["prep"], 7)
            dve.scalar_tensor_tensor(out=tmp[:, 0, :], in0=tmp[:, 1, :], scalar=K_MAX,
                                     in1=coef[:, 0].rearrange("p h t -> p (h t)"), op0=ALU.mult,
                                     op1=ALU.mult).then_inc(s["prep"], 1)
            dve.wait_ge(s["prep"], 8)
            for c in (2, 3):
                dve.tensor_scalar(coef[:, c].rearrange("p h t -> p (h t)"), tmp[:, 0, :], 1.0, None,
                                  ALU.add).then_inc(s["prep"], 1)
            dve.wait_ge(s["prep"], 10)
            dve.wait_ge(s["id_stored"], 16)
            with dve.Fori(0, P // SLOTS) as i:
                for j in range(SLOTS):
                    h, q = divmod(j, STEPS)
                    if q == 0:
                        dve.wait_ge(s["a_ready"], 2 * i + h + 1)
                        dve.wait_ge(stored[h], 16 * i + 16)
                    last = X[:, (j - 1) % SLOTS]
                    now = X[:, j]
                    n0 = SLOTS * 4 * i + 4 * j + 1
                    dve.wait_ge(rec, n0)
                    dve.tensor_tensor(t1[:].rearrange("p (c n) -> p c n", c=2),
                                      a[:, h, q].unsqueeze(1).broadcast_to([P, 2, HN]),
                                      last[:, 2 * HN:4 * HN].rearrange("p (c n) -> p c n", c=2),
                                      ALU.mult).then_inc(rec, 1)
                    ct = coef_r[:, :, bass.ds(SLOTS * i + j, 1)].broadcast_to([P, 4 * G4, N])
                    dve.tensor_tensor(t23[:].rearrange("p (c n) -> p c n", n=N), ct,
                                      last[:, 0:4 * HN].rearrange("p (c n) -> p c n", n=N), ALU.mult).then_inc(rec, 1)
                    dve.wait_ge(rec, n0 + 1)
                    dve.tensor_tensor(now[:, 0:2 * HN], last[:, 0:2 * HN], t1[:], ALU.subtract).then_inc(rec, 1)
                    dve.wait_ge(rec, n0 + 2)
                    ins_ = dve.tensor_tensor(now[:, 2 * HN:4 * HN], t23[:, 0:2 * HN], t23[:, 2 * HN:4 * HN], ALU.add)
                    ins_.then_inc(rec, 1)
            dve.wait_ge(s["det"], 2 * (P // SLOTS) + 1)
            dve.wait_ge(rec, 4 * P + 1)
            end = X[:, SLOTS - 1]
            for row in range(2):
                for pair in range(2):
                    e = end[:, 2 * row * HN:(2 * row + 2) * HN].rearrange("p (c q h n) -> p q h c n", c=2, q=2, h=2)
                    dd = end[:, 4 * HN:5 * HN].rearrange("p (q h n) -> p q h n", q=2, h=2)[:, pair]
                    dve.tensor_tensor(phi[:, pair, row].rearrange("p (h c n) -> p h c n", h=2, c=2), e[:, pair],
                                      dd.unsqueeze(2).broadcast_to([P, 2, 2, N]), ALU.mult).then_inc(s["phi"], 1)
            ent = m["enter"]
            dve.memset(ent[:], 0.0).then_inc(s["phi_done"], 1)
            dve.wait_ge(s["phi_done"], 1)
            dve.wait_ge(s["phiT"], 4)
            dst = ent[:].rearrange("p q g (b c) -> p q g b c", c=TPB)
            srcT = k.bank[0][:].rearrange("p (q g b c) -> p q g b c", q=4, g=HG, b=B)
            for q in range(4):
                for b in range(B):
                    dve.tensor_copy(dst[:, q, :, b, 1:TPB], srcT[:, q, :, b, 0:TPB - 1]).then_inc(s["phi_done"], 1)

        @block.tensor
        def _(pe):
            for q in range(4):
                pe.wait_ge(s["phi"], 4)
                pe.transpose(k.bank[0][:, q * P:(q + 1) * P], phi[:, q // 2, q % 2, :], k.ident[:]).then_inc(s["phiT"], 1)

        @block.gpsimd
        def _(pool):
            pool.sem_inc(s["det"], 1)
            pool.memset(g[:, 1, STEPS], 1.0).then_inc(s["g1"], 1)
            pool.wait_ge(s["prep"], 10)
            pool.wait_ge(s["aexp"], 1)
            pool.wait_ge(s["g1"], 1)

            def a_block(i, h):
                dt = coef[:, 0, :, bass.ds(SLOTS * i + h * STEPS, STEPS)].rearrange("p h t -> p t h")
                Ab = A[:].rearrange("p (h n) -> p h n", n=N).unsqueeze(1).broadcast_to([P, STEPS, G4, N])
                pool.tensor_tensor(a[:, h % 2].rearrange("p t (h n) -> p t h n", n=N),
                                   dt.unsqueeze(3).broadcast_to([P, STEPS, G4, N]), Ab, ALU.mult).then_inc(s["a_ready"], 1)

            def block_of(i, h, last):
                blk = 2 * i + h
                dt = coef[:, 0, :, bass.ds(SLOTS * i + h * STEPS, STEPS)].rearrange("p h t -> p t h")
                f = coef[:, 2, :, bass.ds(SLOTS * i + h * STEPS, STEPS)].rearrange("p h t -> p t h")
                gh = g[:, h, 1:].rearrange("p t (h n) -> p t h n", n=N)
                pool.wait_ge(s["a_ready"], blk + 1)
                wait_alone(pool, s["det"], blk + 1, s["pool_passed"])
                pool.tensor_tensor(gh, dt.unsqueeze(3).broadcast_to([P, STEPS, G4, N]),
                                   a[:, h].rearrange("p t (h n) -> p t h n", n=N), ALU.mult).then_inc(s["g1"], 1)
                wait_alone(pool, s["g1"], 2 * blk + 2, s["pool_passed"])
                pool.tensor_tensor(gh, gh, f.unsqueeze(3).broadcast_to([P, STEPS, G4, N]), ALU.add).then_inc(s["g1"], 1)
                pool.wait_ge(s["g1"], 2 * blk + 3)
                for q in range(STEPS):
                    before = g[:, 1 - h, STEPS] if q == 0 else g[:, h, q]
                    pool.tensor_tensor(g[:, h, q + 1], g[:, h, q + 1], before, ALU.mult).then_inc(s["g_ready"], 1)
                    pool.wait_ge(s["g_ready"], STEPS * blk + q + 1)
                if not last:
                    wait_alone(pool, s["rec"], 4 * STEPS * blk + 1, s["pool_passed"])
                    a_block(i, h + 1)
                pool.wait_ge(s["d0"], blk + 1)
                wait_alone(pool, stored[h], 16 * i + 16, s["pool_passed"])
                dd = X[:, h * STEPS:(h + 1) * STEPS, 4 * HN:5 * HN]
                pool.tensor_tensor(dd, g[:, h, 1:], d0[:], ALU.mult).then_inc(s["n1"], 1)
                wait_alone(pool, s["n1"], blk + 1, s["pool_passed"])
                pool.tensor_scalar(dd, dd, -1.0, 2.0, ALU.mult, ALU.add).then_inc(s["n2"], 1)
                pool.wait_ge(s["n2"], blk + 1)
                pool.tensor_tensor(dd, dd, d0[:], ALU.mult).then_inc(s["det"], 1)
                pool.wait_ge(s["det"], blk + 2)

            a_block(0, 0)
            with pool.Fori(0, P // SLOTS - 1) as i:
                for h in range(2):
                    block_of(i, h, False)
            for h in range(2):
                block_of(P // SLOTS - 1, h, h == 1)


def mix(k, m, ins, scratch):
    nc = k.nc
    BODY = 2 * HG
    LOOPS = TILES // 2
    RING = 4
    with ExitStack() as ctx:
        sb, sem = tools(nc, ctx)
        w_bc = sb("w_bc", P, 2, 4 * N * H)
        vt = sb("vt", P, 2, 2, P)
        pt = sb("pt", P, 2, HG, REC)
        ps = sb("ps", P, 2, HG, 2 * HN)
        sq = sb("sq", P, 2, 4 * HN)
        ss = sb("ss", P, 2, 4 * G4)
        nr = sb("nr", P, 2, 4 * G4)
        rn = sb("rn", P, 4 * G4)
        sc = sb("sc", P, 4, HN)
        cd = sb("cd", P, 2, HN)
        pp = sb("pp", P, 2, 2, 2, HN)
        qq = sb("qq", P, 4, HN)
        cb = sb("cb", P, 4, 2, G4, 2 * N)
        qk = sb("qk", P, 4, 2, 2, P)
        pm = sb("pm", P, 2, 2, 2, P)
        gs = sb("gs", P, 2 * HG, 2, DH)
        tk = sb("tk", P, 2, 2 * HG, 2 * DH)
        hst = sb("hst", P, 2 * HG, 2, DH)
        route = sb("route", P, 2, 2, 2, N)
        s = {n: sem("mx_" + n) for n in (
            "w_loaded", "staged", "bc_ready", "bc_squared", "reduced", "rooted", "rn", "bc_scaled", "cd", "pp", "q1",
            "q2", "ct", "bt", "cb_ready", "tp_ready", "qk_copied", "g_ready", "s_ready", "s_copied", "masked", "y_unit",
            "y_copied", "gs", "state_ready", "r_ready", "h_ready", "init", "pool_passed", "sp_passed")}
        t_loaded = [sem(f"mx_tl{h}") for h in range(2)]
        BC, TP, SE, SO, YB, GB = k.bank[0:2], k.bank[2:4], k.bank[4], k.bank[5], k.bank[6], k.bank[7]
        block = ctx.enter_context(nc.Block())

        def run(eng, step, first, most):
            for n in range(first, 0):
                step(0, n, 0, BODY)
            with eng.Fori(0, LOOPS - 1) as i:
                for n in range(BODY):
                    step(i, n, 0, BODY + most)
            for n in range(BODY):
                step(LOOPS - 1, n, 0, BODY)

        psi = scratch["psi"].rearrange("(g c) t f -> c t g f", g=HG)

        @block.sync
        def _(sp):
            sp.dma_start(w_bc[:], ins["w_bc"].rearrange("(c p) o -> p c o", p=P)).then_inc(s["w_loaded"], 16)

            def load(t, h):
                sp.dma_start(pt[:, h], psi[t, 1:P + 1]).then_inc(t_loaded[h], 16)
                sp.dma_start(ps[:, h], psi[t, 0:P, :, 2 * HN:4 * HN]).then_inc(t_loaded[h], 16)

            load(0, 0)
            load(1, 1)
            with sp.Fori(0, LOOPS - 1) as i:
                for h in range(2):
                    wait_alone(sp, s["cb_ready"], BODY * i + HG * (h + 1), s["sp_passed"])
                    wait_alone(sp, s["ct"], BODY * i + HG * (h + 1) + 2, s["sp_passed"])
                    sp.dma_start(pt[:, h], psi[bass.ds(2 * i + 2 + h, 1), 1:P + 1].rearrange("c t g f -> (c t) g f")
                                 ).then_inc(t_loaded[h], 16)
                    sp.dma_start(ps[:, h], psi[bass.ds(2 * i + 2 + h, 1), 0:P, :, 2 * HN:4 * HN].rearrange(
                        "c t g f -> (c t) g f")).then_inc(t_loaded[h], 16)

        @block.tensor
        def _(pe):
            def tile_slice(ap, i, n, lo, w):
                return ap[:, 2 * i + n // HG, lo:lo + w]

            def step(i, n, lo, hi):
                unit = BODY * i
                if lo <= n < hi and n < BODY:
                    hg = n % HG
                    pe.wait_ge(s["masked"], unit + n + 1)
                    if hg == 0:
                        pe.wait_ge(s["h_ready"], 2 * (2 * i + n // HG) + 3)
                        pe.wait_ge(s["y_copied"], 2 * i + n // HG + 1)
                    for pair in range(2):
                        c0 = (2 * hg + pair) * 2 * DH
                        pe.matmul(YB[:, c0:c0 + 2 * DH], qk[:, n % RING, 0, pair], hst[:, 2 * hg + pair],
                                  start=True, stop=False)
                        for h in range(2):
                            y = pe.matmul(YB[:, c0 + h * DH:c0 + (h + 1) * DH], pm[:, n % 2, h, pair],
                                          tile_slice(m["u"], i, n, c0 + h * DH, DH), start=False, stop=(h == 1))
                    y.then_inc(s["y_unit"], 1)
                if lo <= n + 2 < hi:
                    q = n + 2
                    pe.wait_ge(s["qk_copied"], unit + q + 1)
                    if not (isinstance(i, int) and i == 0 and q < 1):
                        pe.wait_ge(s["s_copied"], 2 * (unit + q))
                    if lo <= n + 1 < hi and (n + 1) % HG == 0:
                        pe.wait_ge(s["state_ready"], 2 * i + (n + 1) // HG + 1)
                        for r in range(2):
                            mm = pe.matmul(SE[:, 256:512], route[:, r].rearrange("p h r n -> p (h r n)"),
                                           tk[:, r].rearrange("p g d -> p (g d)"), start=(r == 0), stop=(r == 1))
                        mm.then_inc(s["r_ready"], 1)
                    for pair in range(2):
                        for h in range(2):
                            lane = slice(64 * h, 64 * h + 64)
                            mm = pe.matmul((SE, SO)[h][:, pair * P:(pair + 1) * P], qk[lane, q % RING, 1, pair],
                                           qk[lane, q % RING, 0, pair])
                    mm.then_inc(s["s_ready"], 1)
                if lo <= n + 5 < hi:
                    q = n + 5
                    if not (isinstance(i, int) and i == 0 and q < 2):
                        pe.wait_ge(s["bc_squared"], unit + q - 1)
                        pe.wait_ge(s["bc_scaled"], unit + q - 1)
                    if q % HG == 0:
                        pe.wait_ge(s["staged"], 2 * i + q // HG + 1)
                    for c in range(2):
                        mm = pe.matmul(BC[q % 2][:], vt[:, q // HG % 2, c], w_bc[:, c, q % HG * 4 * HN:(q % HG + 1) * 4 * HN],
                                       start=(c == 0), stop=(c == 1))
                    mm.then_inc(s["bc_ready"], 1)
                if lo <= n + 3 < hi:
                    q = n + 3
                    pe.wait_ge(s["cb_ready"], unit + q + 1)
                    if not (isinstance(i, int) and i == 0 and q < 2):
                        pe.wait_ge(s["qk_copied"], unit + q - 1)
                    for which in (1, 0):
                        if which == 0:
                            pe.wait_ge(s["ct"], unit + q + 3)
                        for pair in range(2):
                            c0 = (2 * which + pair) * P
                            mm = pe.transpose(TP[q % 2][:, c0:c0 + P],
                                              cb[:, q % RING, which, 2 * pair:2 * pair + 2].rearrange("p h n -> p (h n)"),
                                              k.ident[:])
                    mm.then_inc(s["tp_ready"], 1)
                if lo <= n + 2 < hi:
                    q = n + 2
                    if q % HG == 0:
                        pe.wait_ge(s["gs"], 2 * i + q // HG + 1)
                    for pair in range(2):
                        c0 = (2 * (q % HG) + pair) * 2 * DH
                        mm = pe.matmul(GB[:, c0:c0 + 2 * DH],
                                       cb[:, q % RING, 1, 2 * pair:2 * pair + 2].rearrange("p h n -> p (h n)"),
                                       tile_slice(m["u"], i, q, c0, 2 * DH))
                    mm.then_inc(s["g_ready"], 1)

            for name in ("tp_ready", "g_ready", "y_unit"):
                pe.sem_inc(s[name], RING)
            pe.wait_ge(s["w_loaded"], 16)
            run(pe, step, -5, 5)

        @block.scalar
        def _(act):
            def step(i, n, lo, hi):
                unit = BODY * i
                if lo <= n < hi and n < BODY and n % HG == HG - 1:
                    t = 2 * i + n // HG
                    act.wait_ge(s["y_unit"], unit + n + 1 + RING)
                    act.copy(m["y"][:, t, :], YB[:, 0:DI]).then_inc(s["y_copied"], 1)
                if lo <= n + 2 < hi:
                    q = n + 2
                    act.wait_ge(s["s_ready"], unit + q + 1)
                    act.wait_ge(s["y_unit"], unit + q + RING - 1)
                    for h in range(2):
                        act.copy(pm[:, q % 2, h].rearrange("p a t -> p (a t)"), (SE, SO)[h][:, 0:2 * P]
                                 ).then_inc(s["s_copied"], 1)
                if lo <= n + 1 < hi and (n + 1) % HG == 0:
                    t = 2 * i + (n + 1) // HG
                    act.wait_ge(s["r_ready"], t + 1)
                    act.wait_ge(s["gs"], t + 1)
                    for h in range(2):
                        lane = slice(64 * h, 64 * h + 64)
                        act.copy(hst[lane, :, h, :], SE[lane, 256:512].rearrange("p (g h d) -> p g h d", h=2, d=DH)[:, :, h]
                                 ).then_inc(s["h_ready"], 1)
                if lo <= n + 5 < hi:
                    q = n + 5
                    act.wait_ge(s["bc_ready"], unit + q + 1)
                    if not (isinstance(i, int) and i == 0 and q < 2):
                        act.wait_ge(s["reduced"], unit + q - 1)
                    act.activation(sq[:, q % 2], BC[q % 2][:], ACT.Square).then_inc(s["bc_squared"], 1)
                if lo <= n + 4 < hi:
                    q = n + 4
                    act.wait_ge(s["reduced"], unit + q + 1)
                    if not (isinstance(i, int) and i == 0 and q < 2):
                        act.wait_ge(s["rn"], 3 * (unit + q - 2) + 2)
                    act.activation(nr[:, q % 2], ss[:, q % 2], ACT.Sqrt).then_inc(s["rooted"], 1)
                if lo <= n + 3 < hi:
                    q = n + 3
                    act.wait_ge(s["tp_ready"], unit + q + 1 + RING)
                    act.wait_ge(s["y_unit"], unit + q + 1)
                    act.copy(qk[:, q % RING].rearrange("p a b t -> p (a b t)"), TP[q % 2][:]).then_inc(s["qk_copied"], 1)

            act.sem_inc(s["y_copied"], 1)
            act.wait_ge(s["init"], 2)
            act.sem_inc(s["h_ready"], 1)
            run(act, step, -5, 5)

        @block.vector
        def _(dve):
            dve.memset(hst[:], 0.0).then_inc(s["init"], 1)
            dve.memset(GB[:, 0:256], 0.0).then_inc(s["init"], 1)
            dve.memset(route[:], 0.0).then_inc(s["init"], 1)
            dve.wait_ge(s["init"], 3)
            idr = k.ident[:].rearrange("p (h c n) -> p h c n", h=2, c=2)
            for r in range(2):
                dve.tensor_tensor(route[:, r, :, r, :], idr[:, :, 0, :], idr[:, :, 1, :], ALU.add).then_inc(s["init"], 1)
            dve.wait_ge(s["init"], 5)

            def reduce(i, q):
                unit = BODY * i
                dve.wait_ge(s["bc_squared"], unit + q + 1)
                if not (isinstance(i, int) and i == 0 and q < 2):
                    dve.wait_ge(s["rooted"], unit + q - 1)
                dve.tensor_reduce(ss[:, q % 2], sq[:, q % 2].rearrange("p (a n) -> p a n", n=N), AX.X,
                                  ALU.add).then_inc(s["reduced"], 1)

            def step(i, n, lo, hi):
                u = BODY * i + n
                h, hg = n // HG % 2, n % HG
                if n >= 0:
                    dve.wait_ge(s["rooted"], u + 1)
                    dve.tensor_scalar(nr[:, n % 2], nr[:, n % 2], NORM_EPS, None, ALU.add).then_inc(s["rn"], 1)
                    dve.wait_ge(s["rn"], 3 * u + 1)
                    dve.reciprocal(rn[:], nr[:, n % 2]).then_inc(s["rn"], 1)
                    dve.wait_ge(s["rn"], 3 * u + 2)
                    rb = rn[:].rearrange("p (h c) -> p h c", c=4)
                    dt = m["dt"][:, 2 * i + n // HG, hg * G4:(hg + 1) * G4].unsqueeze(2).broadcast_to([P, G4, 2])
                    dve.tensor_tensor(rb[:, :, 0:2], rb[:, :, 0:2], dt, ALU.mult).then_inc(s["rn"], 1)
                    dve.wait_ge(s["bc_ready"], u + 1)
                    dve.wait_ge(s["rn"], 3 * u + 3)
                    dve.tensor_tensor(sc[:].rearrange("p c (h n) -> p h c n", n=N),
                                      BC[n % 2][:].rearrange("p (h c n) -> p h c n", c=4, n=N),
                                      rb.unsqueeze(3).broadcast_to([P, G4, 4, N]), ALU.mult).then_inc(s["bc_scaled"], 1)
                if lo <= n + 1 < hi:
                    reduce(i, n + 1)
                if n < 0:
                    return
                if hg == 0:
                    dve.wait_ge(t_loaded[h], 32 * i + 32)
                dve.wait_ge(s["bc_scaled"], u + 1)
                z = pt[:, h, hg, :]
                dve.tensor_tensor(qq[:, 0:2], sc[:, 0:1].broadcast_to([P, 2, HN]),
                                  ps[:, h, hg].rearrange("p (c n) -> p c n", n=HN), ALU.mult).then_inc(s["q1"], 1)
                dve.tensor_tensor(qq[:, 2:4], sc[:, 1:2].broadcast_to([P, 2, HN]),
                                  z[:, 0:2 * HN].rearrange("p (c n) -> p c n", n=HN), ALU.mult).then_inc(s["q2"], 1)
                dve.wait_ge(s["cd"], u + 1)
                dve.wait_ge(s["ct"], u + 1)
                dve.tensor_tensor(pp[:, n % 2], cd[:].unsqueeze(2).broadcast_to([P, 2, 2, HN]),
                                  z[:, 0:4 * HN].rearrange("p (r c n) -> p r c n", r=2, c=2), ALU.mult).then_inc(s["pp"], 1)
                dve.wait_ge(s["q2"], u + 1)
                dve.wait_ge(s["tp_ready"], u + 1)
                dve.wait_ge(s["g_ready"], u + 1)
                dst = cb[:, n % RING, 1].rearrange("p h (c n) -> p c h n", c=2)
                qv = qq[:].rearrange("p c (h n) -> p c h n", n=N)
                dve.tensor_tensor(dst[:, 0], qv[:, 1], qv[:, 3], ALU.subtract).then_inc(s["bt"], 1)
                dve.wait_ge(s["bt"], u + 1)
                dve.tensor_tensor(dst[:, 1], qv[:, 2], qv[:, 0], ALU.subtract).then_inc(s["cb_ready"], 1)
                dve.wait_ge(s["cb_ready"], u + 1)
                if hg == 1:
                    t = 2 * i + n // HG
                    dve.wait_ge(s["g_ready"], HG * t + RING)
                    dve.wait_ge(s["h_ready"], 2 * t + 1)
                    dve.tensor_tensor(gs[:].rearrange("p g h d -> p (g h d)"), hst[:].rearrange("p g h d -> p (g h d)"),
                                      GB[:, 0:256], ALU.add).then_inc(s["gs"], 1)
                    dve.wait_ge(s["gs"], t + 1)
                    for r in range(2):
                        e = m["enter"][:].rearrange("p (q r) g t -> p r g q t", r=2)[:, r, :, :, t]
                        ins_ = dve.tensor_tensor(
                            tk[:, r].rearrange("p (g q) d -> p g q d", q=2),
                            gs[:].rearrange("p (g q) h d -> p g q (h d)", q=2),
                            e.unsqueeze(3).broadcast_to([P, HG, 2, 2 * DH]), ALU.mult)
                        if r == 1:
                            ins_.then_inc(s["state_ready"], 1)

            run(dve, step, -1, 1)

        @block.gpsimd
        def _(pool):
            def stage(i, t):
                pool.tensor_copy(vt[:, t % 2], m["valueT"][:, :, bass.ds((2 * i + t) * P, P)]).then_inc(s["staged"], 1)

            def step(i, n, lo, hi):
                unit = BODY * i
                if lo <= n + 3 < hi:
                    q = n + 3
                    h, hg = q // HG % 2, q % HG
                    if hg == 0:
                        pool.wait_ge(t_loaded[h], 32 * i + 32 * (q // BODY) + 32)
                    pool.wait_ge(s["bc_scaled"], unit + q + 1)
                    if not (isinstance(i, int) and i == 0 and q < 1):
                        pool.wait_ge(s["pp"], unit + q)
                    pool.tensor_tensor(cd[:], sc[:, 2:4], pt[:, h, hg, 4 * HN:].unsqueeze(1).broadcast_to([P, 2, HN]),
                                       ALU.mult).then_inc(s["cd"], 1)
                    pool.wait_ge(s["pp"], unit + q + 1)
                    pool.wait_ge(s["tp_ready"], unit + q + 1)
                    pool.tensor_tensor(cb[:, q % RING, 0].rearrange("p h (c n) -> p c h n", c=2),
                                       pp[:, q % 2, 0].rearrange("p c (h n) -> p c h n", n=N),
                                       pp[:, q % 2, 1].rearrange("p c (h n) -> p c h n", n=N), ALU.add).then_inc(s["ct"], 1)
                if lo <= n + 2 < hi:
                    q = n + 2
                    wait_alone(pool, s["s_copied"], 2 * (unit + q) + 2, s["pool_passed"])
                    v = pm[:, q % 2].rearrange("p a b t -> p (a b) t")
                    pool.affine_select(out=v, in_=v, compare_op=ALU.is_ge, fill=0.0, base=0, pattern=[[0, 4], [1, P]],
                                       channel_multiplier=-1).then_inc(s["masked"], 1)
                if n >= 0 and n % HG == 0 and n + 8 < hi:
                    wait_alone(pool, s["bc_ready"], unit + n // HG * HG + 1, s["pool_passed"])
                    stage(i, n // HG + 1)

            pool.sem_inc(s["ct"], 2)
            stage(0, 0)
            run(pool, step, -3, 16)


def close(k, m, ins):
    nc = k.nc
    with ExitStack() as ctx:
        sb, sem = tools(nc, ctx)
        w = sb("w_out", P, 2, D)
        skip = sb("skip", P, DI)
        yT = sb("yT", P, 4, 2, P)
        s = {n: sem("cl_" + n) for n in ("loaded", "sk", "sum", "y", "yT_ready", "yT_taken", "o_ready", "x")}
        block = ctx.enter_context(nc.Block())

        @block.sync
        def _(sp):
            sp.dma_start(w[:], ins["w_out"].rearrange("(c p) d -> p c d", p=P)).then_inc(s["loaded"], 16)
            sp.dma_start(skip[:], ins["skip"].rearrange("(a c) -> a c", a=1).broadcast_to([P, DI])).then_inc(s["loaded"], 16)

        @block.vector
        def _(dve):
            dve.wait_ge(s["loaded"], 32)

            def residual(t):
                dve.wait_ge(s["o_ready"], t + 1)
                dve.tensor_tensor(k.x[:, t, :], k.x[:, t, :], k.bank[4 + t % 4][:, 0:D], ALU.add).then_inc(s["x"], 1)

            for t in range(TILES):
                dve.tensor_tensor(m["u"][:, t], m["u"][:, t], skip[:], ALU.mult).then_inc(s["sk"], 1)
                dve.wait_ge(s["sk"], t + 1)
                dve.tensor_tensor(m["y"][:, t], m["y"][:, t], m["u"][:, t], ALU.add).then_inc(s["sum"], 1)
                dve.wait_ge(s["sum"], t + 1)
                dve.tensor_tensor(m["y"][:, t], m["y"][:, t], m["gate"][:, t], ALU.mult).then_inc(s["y"], 1)
                if t >= 2:
                    residual(t - 2)
            residual(TILES - 2)
            residual(TILES - 1)

        @block.tensor
        def _(pe):
            def turn(t):
                pe.wait_ge(s["y"], t + 1)
                if t >= 4:
                    pe.wait_ge(s["yT_taken"], t - 3)
                for c in range(2):
                    mm = pe.transpose(k.bank[t % 4][:, c * P:(c + 1) * P], m["y"][:, t, c * P:(c + 1) * P], k.ident[:])
                mm.then_inc(s["yT_ready"], 1)

            pe.wait_ge(s["loaded"], 32)
            turn(0)
            for t in range(TILES):
                if t + 1 < TILES:
                    turn(t + 1)
                pe.wait_ge(s["yT_taken"], t + 1)
                if t >= 4:
                    pe.wait_ge(s["x"], t - 3)
                for c in range(2):
                    mm = pe.matmul(k.bank[4 + t % 4][:, 0:D], yT[:, t % 4, c], w[:, c], start=(c == 0), stop=(c == 1))
                mm.then_inc(s["o_ready"], 1)

        @block.scalar
        def _(act):
            for t in range(TILES):
                act.wait_ge(s["yT_ready"], t + 1)
                if t >= 4:
                    act.wait_ge(s["o_ready"], t - 3)
                act.copy(yT[:, t % 4].rearrange("p c t -> p (c t)"), k.bank[t % 4][:, 0:2 * P]).then_inc(s["yT_taken"], 1)


def ffn(k, ins, tag):
    nc = k.nc
    KH = HID // P
    PAIRS = B // 2
    with ExitStack() as ctx:
        sb, sem = tools(nc, ctx)
        xnT = sb(f"xnT{tag}", P, TOK)
        w12 = sb(f"w12{tag}", P, 2, HID)
        h12 = sb(f"h12{tag}", P, 2, KH, HID)
        w3 = sb(f"w3{tag}", P, KH, D)
        s12 = sb(f"s12{tag}", P, 4, KH)
        s3 = sb(f"s3{tag}", P, D)
        g = sb(f"g{tag}", P, 2, T)
        ha = sb(f"ha{tag}", P, 2, KH, T)
        hb = sb(f"hb{tag}", P, 2, KH, T)
        o = sb(f"o{tag}", P, 4, D)
        s = {n: sem(f"{n}{tag}") for n in (
            "loaded", "up_ready", "silu", "gated", "h1_ready", "gelu1", "h2_ready", "gelu2", "out_ready", "scaled", "added")}
        norm_transpose(k, xnT, "f" + tag)
        block = ctx.enter_context(nc.Block())

        @block.sync
        def _(sp):
            for j, n in enumerate(("w1", "w2")):
                sp.dma_start(w12[:, j], ins[n]).then_inc(s["loaded"], 16)
            for j, n in enumerate(("h1", "h2")):
                sp.dma_start(h12[:, j], ins[n].rearrange("(c p) o -> p c o", p=P)).then_inc(s["loaded"], 16)
            sp.dma_start(w3[:], ins["w3"].rearrange("(c p) o -> p c o", p=P)).then_inc(s["loaded"], 16)
            sp.dma_start(s12[:], ins["s12"]).then_inc(s["loaded"], 16)
            sp.dma_start(s3[:], ins["s3"].rearrange("(a d) -> a d", a=1).broadcast_to([P, D])).then_inc(s["loaded"], 16)
            sp.wait_ge(s["loaded"], 112)

        @block.tensor
        def _(pe):
            pe.sem_inc(s["out_ready"], 1)
            pe.wait_ge(s["loaded"], 112)
            with pe.Fori(0, PAIRS) as i:
                for j in range(2 * KH):
                    blk, c = divmod(j, KH)
                    if j < 4:
                        pe.wait_ge(s["gelu2"], 8 * i + 1)
                        pe.wait_ge(s["added"], 2 * i + 1)
                    else:
                        pe.wait_ge(s["gated"], 8 * i + j - 3)
                    for w in range(2):
                        mm = pe.matmul(k.bank[2 * (j % 4) + w][:], w12[:, w, c * P:(c + 1) * P],
                                       xnT[:, bass.ds((2 * i + blk) * T, T)])
                    mm.then_inc(s["up_ready"], 1)
                for layer, (src, before, ready) in enumerate(((ha, "gated", "h1_ready"), (hb, "gelu1", "h2_ready"))):
                    for j in range(2 * KH):
                        blk, c = divmod(j, KH)
                        first = max(KH * (blk + 1), j // 2 + 5) if layer == 0 else KH * (blk + 1) + 1
                        pe.wait_ge(s[before], 8 * i + first)
                        for q in range(KH):
                            mm = pe.matmul(k.bank[j][:], h12[:, layer, q, c * P:(c + 1) * P], src[:, blk, q],
                                           start=(q == 0), stop=(q == KH - 1))
                        mm.then_inc(s[ready], 1)
                for blk in range(2):
                    pe.wait_ge(s["gelu2"], 8 * i + KH * (blk + 1) + 1)
                    for t in range(TPB):
                        for q in range(KH):
                            mm = pe.matmul(k.bank[blk][:, t * D:(t + 1) * D], ha[:, blk, q, t * P:(t + 1) * P], w3[:, q],
                                           start=(q == 0), stop=(q == KH - 1))
                    mm.then_inc(s["out_ready"], 1)

        @block.scalar
        def _(act):
            act.sem_inc(s["gelu1"], 1)
            act.sem_inc(s["gelu2"], 1)
            act.wait_ge(s["loaded"], 112)
            with act.Fori(0, PAIRS) as i:
                for j in range(2 * KH):
                    act.wait_ge(s["up_ready"], 8 * i + j + 1)
                    act.wait_ge(s["gated"], 8 * i + j - 1) if j >= 2 else act.wait_ge(s["added"], 2 * i + 1)
                    act.activation(g[:, j % 2], k.bank[2 * (j % 4)][:], ACT.Silu,
                                   scale=s12[:, 0, j % KH:j % KH + 1]).then_inc(s["silu"], 1)
                for layer, (dst, ready, done) in enumerate(((hb, "h1_ready", "gelu1"), (ha, "h2_ready", "gelu2"))):
                    for j in range(2 * KH):
                        act.wait_ge(s[ready], 8 * i + j + 1)
                        if layer == 1:
                            act.wait_ge(s["h1_ready"], 8 * i + 8)
                        act.activation(dst[:, j // KH, j % KH], k.bank[j][:], ACT.Gelu,
                                       scale=s12[:, 2 + layer, j % KH:j % KH + 1]).then_inc(s[done], 1)

        @block.vector
        def _(dve):
            dve.sem_inc(s["added"], 1)
            dve.wait_ge(s["loaded"], 112)
            with dve.Fori(0, PAIRS) as i:
                for j in range(2 * KH):
                    dve.wait_ge(s["silu"], 8 * i + j + 1)
                    if j == 0:
                        dve.wait_ge(s["out_ready"], 2 * i + 1)
                    dve.scalar_tensor_tensor(out=ha[:, j // KH, j % KH], in0=k.bank[2 * (j % 4) + 1][:],
                                             scalar=s12[:, 1, j % KH:j % KH + 1], in1=g[:, j % 2], op0=ALU.mult,
                                             op1=ALU.mult).then_inc(s["gated"], 1)
                for blk in range(2):
                    dve.wait_ge(s["out_ready"], 2 * i + blk + 2)
                    dve.wait_ge(s["added"], 2 * i + blk + 1)
                    dve.tensor_tensor(o[:], k.bank[blk][:].rearrange("p (t d) -> p t d", d=D),
                                      s3[:].unsqueeze(1).broadcast_to([P, 4, D]), ALU.mult).then_inc(s["scaled"], 1)
                    dve.wait_ge(s["scaled"], 2 * i + blk + 1)
                    xv = k.x[:, bass.ds((2 * i + blk) * TPB, TPB), :]
                    dve.tensor_tensor(xv, xv, o[:], ALU.add).then_inc(s["added"], 1)


def attention(k, ins):
    ORDER = (3, 0, 2, 1)
    nc = k.nc
    PAIRS = HEADS // 2
    UNITS = PAIRS * TPB
    RING = 4
    with ExitStack() as ctx:
        sb, sem = tools(nc, ctx)
        xT = sb("xT", P, TOK)
        wq = sb("wq", P, INNER)
        wkv = sb("wkv", P, 2 * INNER)
        wo = sb("wo", P, PAIRS, D)
        wg = sb("wg", P, HEADS)
        sg = sb("sg", P, TILES, HEADS)
        tri = sb("tri", P, P)
        xb = sb("xb", P, T)
        v = sb("v", P, TPB, INNER)
        qT = sb("qT", P, 2, T)
        kT = sb("kT", P, 2, T)
        mx = sb("mx", P, 2, 2)
        nm = sb("nm", P, 2, 2)
        sm = sb("sm", P, RING, 2)
        rs = sb("rs", P, 2, 2)
        fac = sb("fac", P, 2, 2)
        pr = sb("pr", P, RING, 2, T)
        prT = sb("prT", P, 2, 2, T)
        attT = sb("attT", P, PAIRS, T)
        s = {n: sem("at_" + n) for n in (
            "loaded", "tri0", "tri", "g_ready", "gate", "staged", "v_ready", "v_copied", "p_ready", "p_copied",
            "s_ready", "masked", "max", "neg", "exped", "scaled", "tr_ready", "tr_copied", "pv_ready", "rec", "fac",
            "pv_copied", "o_ready", "added", "pool_passed")}
        norm_transpose(k, xT, "a", rms_weight=ins["norm_w"])
        S = [[k.bank[0], k.bank[1]], [k.bank[2], k.bank[3]]]
        TR, OB, PJ = [k.bank[4], k.bank[5]], k.bank[6], k.bank[7]
        VB = [k.bank[n] for n in range(4)]
        block = ctx.enter_context(nc.Block())

        @block.sync
        def _(sp):
            sp.dma_start(wq[:], ins["wq"]).then_inc(s["loaded"], 16)
            sp.dma_start(wkv[:], ins["wkv"]).then_inc(s["loaded"], 16)
            sp.dma_start(wo[:], ins["wo"].rearrange("(c p) d -> p c d", p=P)).then_inc(s["loaded"], 16)
            sp.dma_start(wg[:], ins["wg"]).then_inc(s["loaded"], 16)
            sp.wait_ge(s["loaded"], 64)

        @block.gpsimd
        def _(pool):
            pool.memset(tri[:], 0.0).then_inc(s["tri0"], 1)
            pool.wait_ge(s["tri0"], 1)
            pool.affine_select(out=tri[:], in_=tri[:], compare_op=ALU.is_ge, fill=MASKED, base=0, pattern=[[-1, P]],
                               channel_multiplier=1).then_inc(s["tri"], 1)
            with pool.Fori(0, B) as b:
                wait_alone(pool, s["p_ready"], 2 * PAIRS * b + 1, s["pool_passed"])
                pool.tensor_copy(xb[:], xT[:, bass.ds(T * b, T)]).then_inc(s["staged"], 1)

        @block.tensor
        def _(pe):
            pe.sem_inc(s["p_ready"], 1)
            pe.sem_inc(s["pv_ready"], 2)
            pe.wait_ge(s["loaded"], 64)
            for t in range(TILES):
                mm = pe.matmul(k.bank[7][:, t * HEADS:(t + 1) * HEADS], xT[:, t * P:(t + 1) * P], wg[:])
            mm.then_inc(s["g_ready"], 1)
            with pe.Fori(0, B) as b:
                base = UNITS * b

                def projection(pair, which):
                    n = 2 * pair + which
                    pe.wait_ge(s["p_copied"], 2 * PAIRS * b + n + 1)
                    w = (wq, wkv)[which]
                    pe.matmul(PJ[:], w[:, pair * P:(pair + 1) * P], xb[:]).then_inc(s["p_ready"], 1)

                pe.wait_ge(s["staged"], b + 1)
                for j in range(2 * TPB):
                    t, half = divmod(j, 2)
                    if j >= 4:
                        pe.wait_ge(s["v_copied"], 2 * TPB * b + j - 3)
                    pe.matmul(VB[j % 4][:], xb[:, t * P:(t + 1) * P],
                              wkv[:, INNER + half * 512:INNER + (half + 1) * 512]).then_inc(s["v_ready"], 1)
                projection(0, 0)
                projection(0, 1)
                for n in range(UNITS + 3):
                    if n < UNITS:
                        pair, it = n // TPB, ORDER[n % TPB]
                        w = (it + 1) * P
                        if n % TPB == 0:
                            pe.wait_ge(s["p_copied"], 2 * PAIRS * b + 2 * pair + 3)
                        if n < 2:
                            pe.wait_ge(s["v_copied"], 2 * TPB * b + 2 * TPB)
                        pe.wait_ge(s["exped"], 2 * (base + n) + 2)
                        for h in range(2):
                            lane = slice(64 * h, 64 * h + 64)
                            mm = pe.matmul(S[n % 2][h][:, 0:w], qT[lane, pair % 2, it * P:(it + 1) * P],
                                           kT[lane, pair % 2, 0:w])
                        mm.then_inc(s["s_ready"], 1)
                        if n % TPB in (1, 2) and pair + 1 < PAIRS:
                            projection(pair + 1, n % TPB - 1)
                    if 2 <= n < UNITS + 2:
                        q = n - 2
                        it = ORDER[q % TPB]
                        pe.wait_ge(s["scaled"], 2 * (base + q) + 2)
                        pe.wait_ge(s["tr_copied"], 2 * (base + q) + 1)
                        for h in range(2):
                            for j in range(it + 1):
                                mm = pe.transpose(TR[h][:, j * P:(j + 1) * P], pr[:, q % RING, h, j * P:(j + 1) * P],
                                                  k.ident[:])
                        mm.then_inc(s["tr_ready"], 1)
                    if n >= 3:
                        q = n - 3
                        pair, it = q // TPB, ORDER[q % TPB]
                        pe.wait_ge(s["tr_copied"], 2 * (base + q) + 3)
                        pe.wait_ge(s["pv_copied"], base + q + 1)
                        for h in range(2):
                            for j in range(it + 1):
                                c0 = (2 * pair + h) * DHEAD
                                mm = pe.matmul(OB[h * DHEAD:(h + 1) * DHEAD, 0:P], v[:, j, c0:c0 + DHEAD],
                                               prT[:, q % 2, h, j * P:(j + 1) * P], start=(j == 0), stop=(j == it))
                        mm.then_inc(s["pv_ready"], 1)
                pe.wait_ge(s["pv_copied"], base + UNITS + 1)
                for t in range(TPB):
                    if t >= 2:
                        pe.wait_ge(s["added"], TPB * b + t - 1)
                    for c in range(PAIRS):
                        mm = pe.matmul(TR[t % 2][:, 0:D], attT[:, c, t * P:(t + 1) * P], wo[:, c], start=(c == 0),
                                       stop=(c == PAIRS - 1))
                    mm.then_inc(s["o_ready"], 1)

        @block.scalar
        def _(act):
            act.sem_inc(s["exped"], 4)
            act.sem_inc(s["tr_copied"], 1)
            act.sem_inc(s["p_copied"], 1)
            act.wait_ge(s["g_ready"], 1)
            act.activation(sg[:].rearrange("p t h -> p (t h)"), k.bank[7][:, 0:TILES * HEADS], ACT.Sigmoid
                           ).then_inc(s["gate"], 1)
            act.wait_ge(s["gate"], 1)
            with act.Fori(0, B) as b:
                base = UNITS * b

                def projected(pair, which):
                    act.wait_ge(s["p_ready"], 2 * PAIRS * b + 2 * pair + which + 2)
                    if which == 0:
                        act.mul(qT[:, pair % 2], PJ[:], DHEAD ** -0.5).then_inc(s["p_copied"], 1)
                    else:
                        act.copy(kT[:, pair % 2], PJ[:]).then_inc(s["p_copied"], 1)

                for j in range(2 * TPB):
                    act.wait_ge(s["v_ready"], 2 * TPB * b + j + 1)
                    act.copy(v[:, j // 2, j % 2 * 512:(j % 2 + 1) * 512], VB[j % 4][:]).then_inc(s["v_copied"], 1)
                projected(0, 0)
                projected(0, 1)
                for n in range(UNITS + 2):
                    if n >= 2:
                        q = n - 2
                        w = (ORDER[q % TPB] + 1) * P
                        act.wait_ge(s["tr_ready"], base + q + 1)
                        act.wait_ge(s["pv_ready"], base + q + 1)
                        for h in range(2):
                            act.copy(prT[:, q % 2, h, 0:w], TR[h][:, 0:w]).then_inc(s["tr_copied"], 1)
                    if n < UNITS:
                        pair, it = n // TPB, ORDER[n % TPB]
                        w = (it + 1) * P
                        act.wait_ge(s["neg"], base + n + 1)
                        if n >= 4:
                            act.wait_ge(s["tr_ready"], base + n - 3)
                        for h in range(2):
                            act.activation(pr[:, n % RING, h, 0:w], S[n % 2][h][:, 0:w], ACT.Exp,
                                           bias=nm[:, n % 2, h:h + 1],
                                           accum_out=sm[:, n % RING, h:h + 1]).then_inc(s["exped"], 1)
                        if n % TPB in (1, 2) and pair + 1 < PAIRS:
                            projected(pair + 1, n % TPB - 1)

        @block.vector
        def _(dve):
            dve.sem_inc(s["pv_copied"], 1)
            dve.wait_ge(s["tri"], 1)
            dve.wait_ge(s["gate"], 1)
            with dve.Fori(0, B) as b:
                base = UNITS * b
                for n in range(UNITS + 3):
                    if n < UNITS:
                        pair, it = n // TPB, ORDER[n % TPB]
                        w = (it + 1) * P
                        dve.wait_ge(s["s_ready"], base + n + 1)
                        for h in range(2):
                            diag = S[n % 2][h][:, it * P:w]
                            dve.tensor_tensor(diag, diag, tri[:], ALU.add).then_inc(s["masked"], 1)
                        for h in range(2):
                            dve.wait_ge(s["masked"], 2 * (base + n) + 1 + h)
                            dve.tensor_reduce(mx[:, n % 2, h:h + 1], S[n % 2][h][:, 0:w], AX.X, ALU.max).then_inc(s["max"], 1)
                        dve.wait_ge(s["max"], 2 * (base + n) + 2)
                        dve.wait_ge(s["exped"], 2 * (base + n) + 2)
                        dve.tensor_scalar(nm[:, n % 2], mx[:, n % 2], -1.0, None, ALU.mult).then_inc(s["neg"], 1)
                    if n >= 3:
                        q = n - 3
                        pair, it = q // TPB, ORDER[q % TPB]
                        dve.wait_ge(s["pv_ready"], base + q + 3)
                        dve.tensor_copy(attT[:, pair, it * P:(it + 1) * P], OB[:, 0:P]).then_inc(s["pv_copied"], 1)
                    if 1 <= n < UNITS + 1:
                        q = n - 1
                        pair, it = q // TPB, ORDER[q % TPB]
                        w = (it + 1) * P
                        dve.wait_ge(s["exped"], 2 * (base + q) + 6)
                        dve.reciprocal(rs[:, q % 2], sm[:, q % RING]).then_inc(s["rec"], 1)
                        dve.wait_ge(s["rec"], base + q + 1)
                        dve.tensor_tensor(fac[:, q % 2], rs[:, q % 2], sg[:, TPB * b + it, 2 * pair:2 * pair + 2],
                                          ALU.mult).then_inc(s["fac"], 1)
                        dve.wait_ge(s["fac"], base + q + 1)
                        for h in range(2):
                            dve.tensor_scalar(pr[:, q % RING, h, 0:w], pr[:, q % RING, h, 0:w], fac[:, q % 2, h:h + 1],
                                              None, ALU.mult).then_inc(s["scaled"], 1)
                for t in range(TPB):
                    dve.wait_ge(s["o_ready"], TPB * b + t + 1)
                    xv = k.x[:, bass.ds(TPB * b + t, 1), :].rearrange("p a d -> p (a d)")
                    dve.tensor_tensor(xv, xv, TR[t % 2][:, 0:D], ALU.add).then_inc(s["added"], 1)


def store(k, out):
    nc = k.nc
    with ExitStack() as ctx:
        sb, sem = tools(nc, ctx)
        out_stored = sem("out_stored")
        block = ctx.enter_context(nc.Block())

        @block.sync
        def _(sp):
            sp.dma_start(out.rearrange("(t p) d -> p t d", p=P), k.x[:]).then_inc(out_stored, 16)
            sp.wait_ge(out_stored, 16)


def build(nc, a, out, debug):
    with ExitStack() as ctx:
        k = Kernel(nc, ctx, debug)
        psi = nc.dram_tensor("psi", [P, P + 1, REC], F32, kind="ExternalOutput" if debug else "Internal").ap()
        par = nc.dram_tensor("par_scratch", [2 * H, TOK], F32, kind="Internal").ap()
        scratch = {"psi": psi, "par": par}
        load_and_identity(k, a["x"])
        with ExitStack() as mctx:
            sb, sem = tools(nc, mctx)
            m = {"valueT": sb("valueT", P, 2, TOK), "u": sb("u", P, TILES, DI), "gate": sb("gate", P, TILES, DI),
                 "dt": sb("dt", P, TILES, H), "enter": sb("enter", P, 4, HG, TILES)}
            project(k, m, a, scratch)
            recur(k, m, a, scratch)
            m["y"] = sb("y", P, TILES, DI)
            mix(k, m, a, scratch)
            close(k, m, a)
            if debug:
                dump(k, m, out)
        ffn(k, {n: a["f0_" + n] for n in FFN_INS}, "A")
        attention(k, a)
        ffn(k, {n: a["f1_" + n] for n in FFN_INS}, "B")
        store(k, out)


def dump(k, m, out):
    nc = k.nc
    with ExitStack() as ctx:
        sb, sem = tools(nc, ctx)
        d = sem("dumped")
        block = ctx.enter_context(nc.Block())

        @block.sync
        def _(sp):
            n = 0
            for name, t in m.items():
                if name == "valueT": continue
                o = k.nc.dram_tensor("dbg_" + name, list(t.shape), F32, kind="ExternalOutput").ap()
                sp.dma_start(o, t[:]).then_inc(d, 16)
                n += 16
            o = nc.dram_tensor("x1", [P, TILES, D], F32, kind="ExternalOutput").ap()
            sp.dma_start(o, k.x[:]).then_inc(d, 16)
            sp.wait_ge(d, n + 16)


FFN_INS = ("w1", "w2", "h1", "h2", "w3", "s12", "s3")


DEBUG = False


def kernel(**inputs):
    import numpy as np
    import concourse.bacc as bacc
    from concourse.bass_utils import run_bass_kernel_spmd as run

    i = {n: np.ascontiguousarray(v) for n, v in inputs.items()}
    wi = i["L0_attn_W_in"]
    par = wi[2 * DI:].reshape(H, 2, D)
    w_in = np.concatenate([wi[:DI], par[:, 0], par[:, 1], wi[DI:2 * DI]], axis=0)
    arrays = {
        "x": i["L0_attn_x"].reshape(TOK, D),
        "w_in": np.ascontiguousarray(w_in.T),
        "dw": i["L0_attn_dw_weight"],
        "db": np.ascontiguousarray(i["L0_attn_dw_bias"].reshape(2, P).T),
        "w_bc": np.ascontiguousarray(i["L0_attn_W_bc"].T),
        "w_out": np.ascontiguousarray(i["L0_attn_W_out"].T),
        "skip": i["L0_attn_skip"],
        "A_log": i["L0_attn_A_log"],
        "dt_bias": i["L0_attn_dt_bias"],
        "norm_w": i["L1_attn_norm_w"].reshape(D, 1),
        "wq": i["L1_attn_Wq"],
        "wkv": i["L1_attn_Wkv"],
        "wo": i["L1_attn_Wout"],
        "wg": i["L1_attn_Wg"],
    }
    for layer in range(2):
        f = {n: i[f"L{layer}_ffn_{n}"] for n in (w + e for w in ("w1", "w2", "h1", "h2", "w3") for e in ("_w", "_s"))}
        for w in ("w1", "w2", "h1", "h2", "w3"):
            arrays[f"f{layer}_{w}"] = np.ascontiguousarray(f[w + "_w"].T)
        s12 = np.stack([f[w + "_s"].reshape(HID // P, P) for w in ("w1", "w2", "h1", "h2")])
        arrays[f"f{layer}_s12"] = np.ascontiguousarray(s12.transpose(2, 0, 1))
        arrays[f"f{layer}_s3"] = f["w3_s"]
    nc = bacc.Bacc("TRN2", target_bir_lowering=False, num_devices=1)
    aps = {n: nc.dram_tensor("in_" + n, v.shape, F32, kind="ExternalInput").ap() for n, v in arrays.items()}
    out = nc.dram_tensor("out_0", [TOK, D], F32, kind="ExternalOutput").ap()
    build(nc, aps, out, DEBUG)
    r = run(nc, [{"in_" + n: v for n, v in arrays.items()}], core_ids=[0])
    return r.results[0]["out_0"].reshape(B, T, D)
```
